# Optimizing a Trainium2 kernel written in Bass

```python
import numpy as np
import jax
import jax.numpy as jnp

def _softmax(x, axis=-1):
    return jax.nn.softmax(x, axis=axis)

def _gelu(x):
    return jax.nn.gelu(x, approximate=True)

def _silu(x):
    return jax.nn.silu(x)

def _sigmoid(x):
    return jax.nn.sigmoid(x)

def _layernorm(x, axis=-1, eps=1e-05):
    m = jnp.mean(x, axis=axis, keepdims=True)
    v = jnp.var(x, axis=axis, keepdims=True)
    return (x - m) / jnp.sqrt(v + eps)

def _scatter_add(tgt, idx, src, axis=0):
    return tgt.at[idx].add(src)

def _segment_sum(src, seg, n):
    return jax.ops.segment_sum(src, seg, n)
kernel_name = 'mk_seq_postln_d1_jaxref_r4_cda07f'

def setup_inputs(seed: int=0):
    np.random.seed(seed)
    _w = jnp.asarray

    def _L0_attn_setup():
        import jax, jax.numpy as jnp
        import numpy as np
        EMBED_DIM = 256
        VALUE_DIM = 512
        NUM_HEADS = 8
        KEY_DIM = EMBED_DIM // NUM_HEADS
        HEAD_DIM = VALUE_DIM // NUM_HEADS
        EPS = 1e-05
        B, S = (2, 512)

        def _xavier(k, shape, gain):
            a = gain * np.sqrt(6.0 / (shape[0] + shape[1]))
            return jax.random.uniform(k, shape, jnp.float32, -a, a)

        def _rel_pos(slen):
            lin = jnp.linspace(0.0, 1.0, KEY_DIM // 2)
            angle = jnp.repeat(1.0 / 10000.0 ** lin, 2)
            decay = jnp.log1p(-2.0 ** (-5.0 - jnp.arange(NUM_HEADS, dtype=jnp.float32)))
            idx = jnp.arange(slen, dtype=jnp.float32)
            sin = jnp.sin(idx[:, None] * angle[None, :])
            cos = jnp.cos(idx[:, None] * angle[None, :])
            diff = idx[:, None] - idx[None, :]
            m = jnp.where(diff[None] >= 0, jnp.exp(diff[None] * decay[:, None, None]), 0.0)
            m = m / jnp.sqrt(m.sum(-1, keepdims=True))
            return (sin, cos, m)

        def _rotate_every_two(x):
            x1 = x[..., ::2]
            x2 = x[..., 1::2]
            return jnp.stack((-x2, x1), axis=-1).reshape(x.shape)
        key = jax.random.key(seed)
        ks = jax.random.split(key, 6)
        g = 2.0 ** (-2.5)
        return {'x': jax.random.normal(ks[0], (B, S, EMBED_DIM), jnp.float32), 'wq': _xavier(ks[1], (EMBED_DIM, EMBED_DIM), g), 'wk': _xavier(ks[2], (EMBED_DIM, EMBED_DIM), g), 'wv': _xavier(ks[3], (EMBED_DIM, VALUE_DIM), g), 'wg': _xavier(ks[4], (EMBED_DIM, VALUE_DIM), g), 'wo': _xavier(ks[5], (VALUE_DIM, EMBED_DIM), 1.0)}
    _L0_attn_in = _L0_attn_setup()

    def _L0_ffn_setup():
        import jax, jax.numpy as jnp
        import numpy as np
        BEST_K = 2

        def _expert(xf, w1, w3, w2):
            return jax.nn.silu(xf @ w1) * (xf @ w3) @ w2
        key = jax.random.key(seed)
        ks = jax.random.split(key, 9)
        E, S_sh, D, H = (8, 2, 256, 128)
        B, S = (2, 512)
        w = lambda k, shape: jax.random.normal(k, shape, dtype=jnp.float32) * 0.02
        return {'x': jax.random.normal(ks[0], (B, S, D), dtype=jnp.float32), 'router_w': w(ks[1], (D, E)), 'router_b': jnp.zeros((E,), dtype=jnp.float32), 'routed_w1': w(ks[2], (E, D, H)), 'routed_w3': w(ks[3], (E, D, H)), 'routed_w2': w(ks[4], (E, H, D)), 'shared_w1': w(ks[5], (S_sh, D, H)), 'shared_w3': w(ks[6], (S_sh, D, H)), 'shared_w2': w(ks[7], (S_sh, H, D))}
    _L0_ffn_in = _L0_ffn_setup()
    _d = {'L0_attn_x': _L0_attn_in['x'], 'L0_attn_wq': _L0_attn_in['wq'], 'L0_attn_wk': _L0_attn_in['wk'], 'L0_attn_wv': _L0_attn_in['wv'], 'L0_attn_wg': _L0_attn_in['wg'], 'L0_attn_wo': _L0_attn_in['wo'], 'L0_ffn_router_w': _L0_ffn_in['router_w'], 'L0_ffn_router_b': _L0_ffn_in['router_b'], 'L0_ffn_routed_w1': _L0_ffn_in['routed_w1'], 'L0_ffn_routed_w3': _L0_ffn_in['routed_w3'], 'L0_ffn_routed_w2': _L0_ffn_in['routed_w2'], 'L0_ffn_shared_w1': _L0_ffn_in['shared_w1'], 'L0_ffn_shared_w3': _L0_ffn_in['shared_w3'], 'L0_ffn_shared_w2': _L0_ffn_in['shared_w2']}
    _x0 = _d['L0_attn_x']
    _d['L0_attn_x'] = jax.random.normal(jax.random.fold_in(jax.random.key(seed), 1), (8, 1024, 256), dtype=_x0.dtype)
    del _x0
    return _d

def reference(L0_attn_x, L0_attn_wq, L0_attn_wk, L0_attn_wv, L0_attn_wg, L0_attn_wo, L0_ffn_router_w, L0_ffn_router_b, L0_ffn_routed_w1, L0_ffn_routed_w3, L0_ffn_routed_w2, L0_ffn_shared_w1, L0_ffn_shared_w3, L0_ffn_shared_w2):

    def _L0_attn_ref(x, wq, wk, wv, wg, wo):
        import jax, jax.numpy as jnp
        import numpy as np
        EMBED_DIM = 256
        VALUE_DIM = 512
        NUM_HEADS = 8
        KEY_DIM = EMBED_DIM // NUM_HEADS
        HEAD_DIM = VALUE_DIM // NUM_HEADS
        EPS = 1e-05
        B, S = (2, 512)

        def _xavier(k, shape, gain):
            a = gain * np.sqrt(6.0 / (shape[0] + shape[1]))
            return jax.random.uniform(k, shape, jnp.float32, -a, a)

        def _rel_pos(slen):
            lin = jnp.linspace(0.0, 1.0, KEY_DIM // 2)
            angle = jnp.repeat(1.0 / 10000.0 ** lin, 2)
            decay = jnp.log1p(-2.0 ** (-5.0 - jnp.arange(NUM_HEADS, dtype=jnp.float32)))
            idx = jnp.arange(slen, dtype=jnp.float32)
            sin = jnp.sin(idx[:, None] * angle[None, :])
            cos = jnp.cos(idx[:, None] * angle[None, :])
            diff = idx[:, None] - idx[None, :]
            m = jnp.where(diff[None] >= 0, jnp.exp(diff[None] * decay[:, None, None]), 0.0)
            m = m / jnp.sqrt(m.sum(-1, keepdims=True))
            return (sin, cos, m)

        def _rotate_every_two(x):
            x1 = x[..., ::2]
            x2 = x[..., 1::2]
            return jnp.stack((-x2, x1), axis=-1).reshape(x.shape)
        b, s, _ = x.shape
        sin, cos, mask = _rel_pos(s)
        q = x @ wq
        k = x @ wk * KEY_DIM ** (-0.5)
        v = x @ wv
        g = x @ wg
        q = q.reshape(b, s, NUM_HEADS, KEY_DIM).transpose(0, 2, 1, 3)
        k = k.reshape(b, s, NUM_HEADS, KEY_DIM).transpose(0, 2, 1, 3)
        qr = q * cos + _rotate_every_two(q) * sin
        kr = k * cos + _rotate_every_two(k) * sin
        vr = v.reshape(b, s, NUM_HEADS, HEAD_DIM).transpose(0, 2, 1, 3)
        qk = jnp.einsum('bhik,bhjk->bhij', qr, kr) * mask[None]
        denom = jnp.clip(jnp.abs(jax.lax.stop_gradient(qk).sum(-1, keepdims=True)), 1.0, None)
        qk = qk / denom
        out = jnp.einsum('bhij,bhjd->bihd', qk, vr)
        out = out * jax.lax.rsqrt(jnp.mean(out * out, axis=-1, keepdims=True) + EPS)
        out = out.reshape(b, s, VALUE_DIM)
        out = jax.nn.silu(g) * out
        return out @ wo

    def _L0_ffn_ref(x, router_w, router_b, routed_w1, routed_w3, routed_w2, shared_w1, shared_w3, shared_w2):
        import jax, jax.numpy as jnp
        import numpy as np
        BEST_K = 2

        def _expert(xf, w1, w3, w2):
            return jax.nn.silu(xf @ w1) * (xf @ w3) @ w2
        B, S, D = x.shape
        T = B * S
        xf = x.reshape(T, D)
        logits = xf @ router_w + router_b
        topk_vals, topk_idx = jax.lax.top_k(logits, BEST_K)
        sparse = jnp.full_like(logits, -jnp.inf)
        sparse = sparse.at[jnp.arange(T)[:, None], topk_idx].set(topk_vals)
        gates = jax.nn.softmax(sparse, axis=-1)
        routed = jax.vmap(_expert, in_axes=(None, 0, 0, 0))(xf, routed_w1, routed_w3, routed_w2)
        routed_out = jnp.einsum('etd,te->td', routed, gates)
        shared_out = jax.vmap(_expert, in_axes=(None, 0, 0, 0))(xf, shared_w1, shared_w3, shared_w2).sum(axis=0)
        return (routed_out + shared_out).reshape(B, S, D)
    x = L0_attn_x
    x = _layernorm(x + _L0_attn_ref(x, L0_attn_wq, L0_attn_wk, L0_attn_wv, L0_attn_wg, L0_attn_wo), axis=-1)
    x = _layernorm(x + _L0_ffn_ref(x, L0_ffn_router_w, L0_ffn_router_b, L0_ffn_routed_w1, L0_ffn_routed_w3, L0_ffn_routed_w2, L0_ffn_shared_w1, L0_ffn_shared_w3, L0_ffn_shared_w2), axis=-1)
    return x

_drawn_inputs = setup_inputs


def setup_inputs(seed=0):
    import zlib

    import numpy as np

    out = dict(_drawn_inputs(seed))
    spreads = {'L0_ffn_router_b': (0.0, 0.8)}
    factors = {'L0_ffn_router_w': 7.813,
     'L0_ffn_routed_w1': 6.756,
     'L0_ffn_routed_w3': 6.674,
     'L0_ffn_routed_w2': 6.676,
     'L0_ffn_shared_w1': 3.405,
     'L0_ffn_shared_w3': 3.36,
     'L0_ffn_shared_w2': 3.363}
    for name, (base, spread) in spreads.items():
        noise = np.random.default_rng([zlib.crc32(name.encode()), seed]).standard_normal(out[name].shape)
        drawn = base * np.exp(spread * noise) if base else spread * noise
        out[name] = jnp.asarray(drawn.astype(out[name].dtype))
    for name, factor in factors.items():
        out[name] = (out[name] * factor).astype(out[name].dtype)
    return out
```

```python
import math
from contextlib import ExitStack

import numpy as np

import concourse.bass as bass
from concourse import mybir

BATCH, SEQ, D = 8, 1024, 256
HEADS, KD, HD = 8, 32, 64
VD = HEADS * HD
EXPERTS, SHARED, HID = 8, 2, 128
EPS = 1e-5

P = 128
TPG = 4
GPB = SEQ // (P * TPG)
CHUNKS = SEQ // P
NG = BATCH * GPB
GT = TPG * P
KC = D // P
VC = VD // P
HG = HEADS // 4
HE = HD + 1
OW = 4 * HE
NE = SHARED + EXPERTS
EW = KC * HID * 2 + D
PROJ = 3
PAD = 3.0e38

CONST_WIDTHS = [("gamma", 2 * HEADS), ("cos", CHUNKS * KD), ("sin", CHUNKS * KD), ("causal", P),
                ("block", HG * OW), ("gamma_chunk", HG), ("rowsum", CHUNKS * HEADS), ("ident", P)]
CONST_AT, _at = {}, 0
for _name, _width in CONST_WIDTHS:
    CONST_AT[_name] = (_at, _at + _width)
    _at += _width
CONSTS = _at

SLOT = ["QK", "V", "X1T", "G", "LOGITS", "F", "QKT", "F", "SCORES", "F", "OUT", "F", "F", "F", "YT", "F", "WO"]
SLOT_MORE = ["QK", "V", "X1T", "G", "LOGITS", "F", "QKT", "F", "SCORES", "F", "F", "OUT", "F", "F", "F", "YT",
             "F", "WO"]

START = 1


def feed_forward_steps():
    steps = [("H1", 0), ("H3", 0), ("H1", 1), ("H3", 1), ("H1", 2), ("W", 1), ("H3", 2)]
    for i in range(3, NE):
        steps += [("H1", i), ("H3", i), ("W", i - 1)]
    return steps + [("W", NE - 1)]


def slots(with_ffn):
    steps = feed_forward_steps() if with_ffn else []
    out = []
    for t in range(TPG):
        for part in (SLOT_MORE if t % 2 == 0 else SLOT):
            if part == "F":
                if steps:
                    out.append(steps.pop(0))
            elif part in ("X1T", "LOGITS"):
                out.append((part, t - 1))
            else:
                out.append((part, t))
    return out + steps


class Group:

    def __init__(self, b, at):
        self.b, self.at = b, at
        self.p = at % GPB

    def tiles(self, t, per=1):
        return self.b * (per * CHUNKS) + per * (TPG * self.at + t + 1)

    def experts(self, i, per=1):
        return self.b * (per * NE * GPB) + (per * (NE * self.at + i + 1) + START)

    def down(self, i):
        return self.experts(max(i, -1) or 1, 2)

    def groups(self, per=1, k=1):
        return self.b * (per * GPB) + per * (self.at + k)

    def rows(self, per):
        return self.b * per + per * (self.at // GPB + 1)

    def states(self, chunk, per=1, updates=CHUNKS - 1):
        return self.b * (per * updates) + per * (self.at // GPB * updates + chunk)

    def index(self):
        return self.b * GPB + self.at

    def first(self):
        return isinstance(self.b, int) and self.index() == 0

    def before(self, k):
        return Group(self.b, self.at - k)


def positive(value):
    return not isinstance(value, int) or value > 0


def retention_moe_kernel(nc, x, xT, w_att, w_wo, w_ffn, w_router, b_router, consts, out):
    f32, f32r = mybir.dt.float32, mybir.dt.float32r
    ALU, ACT, AX = mybir.AluOpType, mybir.ActivationFunctionType, mybir.AxisListType

    x_v = x.rearrange("(g t p) d -> g p t d", t=TPG, p=P)
    out_v = out.rearrange("(g t p) d -> g p t d", t=TPG, p=P)

    with ExitStack() as ctx:
        def sb(name, shape, dt=f32):
            return ctx.enter_context(nc.sbuf_tensor(name, shape, dt))

        def sem(name):
            return ctx.enter_context(nc.semaphore(name))

        watt_h, watt_l = sb("watt_h", [P, PROJ, KC, 512], f32r), sb("watt_l", [P, PROJ, KC, 512], f32r)
        wo_h, wo_l = sb("wo_h", [P, VC, D], f32r), sb("wo_l", [P, VC, D], f32r)
        wf_h, wf_l = sb("wf_h", [P, NE, EW], f32r), sb("wf_l", [P, NE, EW], f32r)
        wr = sb("wr", [P, KC, EXPERTS])
        br = sb("br", [P, EXPERTS])
        cst = sb("cst", [P, CONSTS])

        def const(name):
            return cst[:, CONST_AT[name][0]:CONST_AT[name][1]]

        gamma = const("gamma")
        cos = const("cos").rearrange("p (c k) -> p c k", c=CHUNKS)
        sin = const("sin").rearrange("p (c k) -> p c k", c=CHUNKS)
        causal = const("causal")
        block_decay = const("block").rearrange("p (g w) -> p g w", g=HG)
        gamma_chunk = const("gamma_chunk")
        rowsum = const("rowsum").rearrange("p (c h) -> p c h", c=CHUNKS)
        ident = const("ident")

        xraw = sb("xraw", [P, KC, GT])
        x_h, x_l = sb("x_h", [P, 2, KC, P], f32r), sb("x_l", [P, 2, KC, P], f32r)
        xres = sb("xres", [P, 2, TPG, D])
        qk_s, qk_c, qk_w = sb("qk_s", [P, 512]), sb("qk_c", [P, 512]), sb("qk_w", [P, 512])
        qk = sb("qk", [P, 2, 512])
        qkT = sb("qkT", [P, 4, P])
        v = sb("v", [P, HEADS, HE])
        gate = sb("gate", [P, VD])
        scores = sb("scores", [P, 4, 2, P])
        state = sb("state", [P, HG, OW])
        state_new = sb("state_new", [P, HG, OW])
        squares = sb("squares", [P, HEADS, HE])
        sumsq, denom = sb("sumsq", [P, HEADS]), sb("denom", [P, HEADS])
        meansq, rms = sb("meansq", [P, HEADS]), sb("rms", [P, HEADS])
        minus_half = sb("minus_half", [P, HEADS])
        gated, y = sb("gated", [P, VD]), sb("y", [P, VD])
        yT_h, yT_l = sb("yT_h", [P, VC, P], f32r), sb("yT_l", [P, VC, P], f32r)
        res = sb("res", [P, D])
        stats, moments = sb("stats", [P, 6]), sb("moments", [P, 2])
        var_eps, rstd = sb("var_eps", [P, 1]), sb("rstd", [P, 1])
        x1 = sb("x1", [P, 2, TPG, D])
        x1T = sb("x1T", [P, KC, P])
        x1_h, x1_l = sb("x1_h", [P, 2, KC, GT], f32r), sb("x1_l", [P, 2, KC, GT], f32r)
        logits = sb("logits", [P, TPG, EXPERTS + 6])
        top8, top2 = sb("top8", [P, TPG, 8]), sb("top2", [P, TPG, 8])
        without = sb("without", [P, TPG, EXPERTS + 6])
        middle, offset = sb("middle", [P, TPG]), sb("offset", [P, TPG, EXPERTS])
        chosen, share = sb("chosen", [P, TPG, EXPERTS]), sb("share", [P, TPG, EXPERTS])
        half_share = sb("half_share", [P, TPG, EXPERTS])
        gates = sb("gates", [P, 2, TPG, EXPERTS])
        act1 = sb("act1", [P, GT])
        hid = sb("hid", [P, 2, GT])
        hid_h, hid_l = sb("hid_h", [P, 2, GT], f32r), sb("hid_l", [P, 2, GT], f32r)
        stats2, moments2 = sb("stats2", [P, TPG, 6]), sb("moments2", [P, TPG, 2])
        var_eps2, rstd2 = sb("var_eps2", [P, TPG]), sb("rstd2", [P, TPG])

        A = ctx.enter_context(nc.psum_tensor("A", [P, 4, 512], f32))
        F = ctx.enter_context(nc.psum_tensor("F", [P, 4, 512], f32))

        s_cst, s_router, s_out = sem("s_cst"), sem("s_router"), sem("s_out")
        s_stage = [sem("s_stage0"), sem("s_stage1")]
        s_xT, s_x = sem("s_xT"), [sem("s_x0"), sem("s_x1")]
        w_high, w_low = sem("w_high"), sem("w_low")
        ready0 = sem("ready0")
        x_high, x_low = sem("x_high"), sem("x_low")
        qk_proj, v_proj, g_proj = sem("qk_proj"), sem("v_proj"), sem("g_proj")
        qk_scaled, qk_cos, qk_sin, qk_rot = sem("qk_scaled"), sem("qk_cos"), sem("qk_sin"), sem("qk_rot")
        v_sb, gate_sb = sem("v_sb"), sem("gate_sb")
        qkT_ps, qkT_sb = sem("qkT_ps"), sem("qkT_sb")
        scores_ps, scores_sb = sem("scores_ps"), sem("scores_sb")
        out_ps, state_ps, state_upd, state_sb = sem("out_ps"), sem("state_ps"), sem("state_upd"), sem("state_sb")
        sq_sb, norm_step, meansq_sb, rms_sb = sem("sq_sb"), sem("norm_step"), sem("meansq_sb"), sem("rms_sb")
        gated_sb, y_sb = sem("gated_sb"), sem("y_sb")
        yT_ps, yT_high, yT_low = sem("yT_ps"), sem("yT_high"), sem("yT_low")
        wo_ps, ln_step, var_sb, rstd_sb, x1_sb = sem("wo_ps"), sem("ln_step"), sem("var_sb"), sem("rstd_sb"), sem("x1_sb")
        held = sem("held")
        x1T_ps, x1T_sb, x1T_high, x1T_low = sem("x1T_ps"), sem("x1T_sb"), sem("x1T_high"), sem("x1T_low")
        logits_ps, logits_sb = sem("logits_ps"), sem("logits_sb")
        route_step, offset_sb, share_sb = sem("route_step"), sem("offset_sb"), sem("share_sb")
        h1_ps, h3_ps, act1_sb, hid_sb, hid_high, hid_low = (sem("h1_ps"), sem("h3_ps"), sem("act1_sb"), sem("hid_sb"),
                                                            sem("hid_high"), sem("hid_low"))
        ffn_ps, sum_sb = sem("ffn_ps"), sem("sum_sb")
        ln2_step, var2_sb, rstd2_sb, result_sb = sem("ln2_step"), sem("var2_sb"), sem("rstd2_sb"), sem("result_sb")

        stage = [x1[:, 1, :, :].rearrange("p t d -> p (t d)"), xres[:, 1, :, :].rearrange("p t d -> p (t d)")]
        parts = []
        for j in range(PROJ):
            parts.append((w_att[j], KC * 512, watt_h[:, j, :, :].rearrange("p k n -> p (k n)"),
                          watt_l[:, j, :, :].rearrange("p k n -> p (k n)")))
        parts.append((w_wo, VC * D, wo_h[:, :, :].rearrange("p k n -> p (k n)"),
                      wo_l[:, :, :].rearrange("p k n -> p (k n)")))
        for i in range(NE):
            parts.append((w_ffn[i], EW, wf_h[:, i, :], wf_l[:, i, :]))
        FIRST_PARTS = PROJ + 1

        def w1(w, i, k):
            return w[:, i, k * HID:(k + 1) * HID]

        def w3(w, i, k):
            return w[:, i, (KC + k) * HID:(KC + k + 1) * HID]

        def w2(w, i):
            return w[:, i, 2 * KC * HID:EW]

        def whole_run(eng, group):
            group(Group(0, 0), None)
            with eng.Fori(0, BATCH - 1) as b:
                group(Group(b, 1), Group(b, 0))
                group(Group(b, 2), Group(b, 1))
            group(Group(BATCH - 1, 1), Group(BATCH - 1, 0))
            group(None, Group(BATCH - 1, 1))

        def parts_of(ga, gf):
            for part, t in (slots(gf is not None) if ga else
                            [("X1T", -1), ("LOGITS", -1)] + feed_forward_steps()):
                if part in ("H1", "H3", "W"):
                    yield part, t, gf
                elif t >= 0:
                    yield part, t, ga
                elif gf is not None:
                    yield part, TPG - 1, gf

        block = ctx.enter_context(nc.Block())

        @block.sync
        def _(sp):
            def load_xT(g):
                if not g.first():
                    sp.wait_ge(x_low, g.before(1).tiles(TPG - 1))
                sp.dma_start(xraw[:, :, :], xT[g.index()]).then_inc(s_xT, 16)

            def load_x(g):
                if positive(g.groups(1, -1)):
                    sp.wait_ge(ln_step, g.before(2).tiles(TPG - 1, 3))
                sp.dma_start(xres[:, g.p, :, :], x_v[g.index()]).then_inc(s_x[g.p], 16)

            def store(g):
                sp.wait_ge(result_sb, g.groups(TPG))
                sp.dma_start(out_v[g.index()], x1[:, g.p, :, :]).then_inc(s_out, 16)

            sp.sem_inc(s_out, START)
            for n, (src, width, _, _) in enumerate(parts):
                if n == 1:
                    load_xT(Group(0, 0))
                    sp.dma_start(cst[:, :], consts).then_inc(s_cst, 16)
                if n == FIRST_PARTS:
                    load_x(Group(0, 0))
                    sp.dma_start(wr[:, :, :], w_router).then_inc(s_router, 16)
                    sp.dma_start(br[:, :], b_router).then_inc(s_router, 16)
                if n == len(parts) - 1:
                    load_xT(Group(0, 1))
                if n >= 2:
                    sp.wait_ge(w_low, n - 1)
                sp.dma_start(stage[n % 2][:, 0:width], src).then_inc(s_stage[n % 2], 16)
            sp.wait_ge(w_low, len(parts))
            load_x(Group(0, 1))

            with sp.Fori(0, BATCH - 1) as b:
                load_xT(Group(b, 2))
                load_x(Group(b, 2))
                store(Group(b, 0))
                load_xT(Group(b, 3))
                load_x(Group(b, 3))
                store(Group(b, 1))
            store(Group(BATCH - 1, 0))
            store(Group(BATCH - 1, 1))
            sp.wait_ge(s_out, 16 * NG + START)

        @block.tensor
        def _(pe):
            def split_product(o, pairs):
                for k, (lhsT, rhs) in enumerate(pairs):
                    last = pe.matmul(o, lhsT, rhs, start=(k == 0), stop=(k == len(pairs) - 1))
                return last

            def project(g, t, j, bank, done):
                q = t % 2
                pairs = [(a[:, q, k, :], w[:, j, k, :]) for a, w in ((x_h, watt_h), (x_h, watt_l), (x_l, watt_h))
                         for k in range(KC)]
                split_product(A[:, bank, :], pairs).then_inc(done, 1)

            def group(ga, gf):
                for part, t, g in parts_of(ga, gf):
                    c = TPG * g.p + t
                    if part == "QK":
                        pe.wait_ge(x_low, g.tiles(t))
                        if g.first() and t == 0:
                            pe.wait_ge(w_low, 1)
                        if positive(g.states(c, HG)):
                            pe.wait_ge(state_sb, g.states(c, HG))
                        project(g, t, 0, 0, qk_proj)
                    elif part == "V":
                        if g.first() and t == 0:
                            pe.wait_ge(w_low, 2)
                        project(g, t, 1, 1, v_proj)
                    elif part == "X1T":
                        pe.wait_ge(x1_sb, g.tiles(t))
                        for k in range(KC):
                            last = pe.transpose(A[:, 3, k * P:(k + 1) * P], x1[:, g.p, t, k * P:(k + 1) * P], ident)
                        last.then_inc(x1T_ps, 1)
                    elif part == "G":
                        if g.first() and t == 0:
                            pe.wait_ge(w_low, 3)
                        if positive(g.tiles(t - 1)):
                            pe.wait_ge(ln_step, g.tiles(t - 1, 3) - 2)
                        project(g, t, 2, 2, g_proj)
                    elif part == "LOGITS":
                        pe.wait_ge(x1T_sb, g.tiles(t))
                        if g.first() and t == 0:
                            pe.wait_ge(s_router, 32)
                        if not (isinstance(g.b, int) and g.index() == NG - 1 and t == TPG - 1):
                            pe.wait_ge(qk_scaled, g.tiles(t + 1))
                        for k in range(KC):
                            last = pe.matmul(A[:, 0, 0:EXPERTS], x1T[:, k, :], wr[:, k, :],
                                             start=(k == 0), stop=(k == KC - 1))
                        last.then_inc(logits_ps, 1)
                    elif part == "QKT":
                        pe.wait_ge(qk_rot, g.tiles(t))
                        if positive(g.tiles(t - 1)):
                            pe.wait_ge(x1T_low, g.tiles(t - 1))
                        for k in range(4):
                            last = pe.transpose(A[:, 3, k * P:(k + 1) * P], qk[:, t % 2, k * P:(k + 1) * P], ident)
                        last.then_inc(qkT_ps, 1)
                    elif part == "SCORES":
                        pe.wait_ge(qkT_sb, g.tiles(t))
                        if positive(g.tiles(t - 1)):
                            pe.wait_ge(logits_sb, g.tiles(t - 1))
                        pe.wait_ge(v_sb, g.tiles(t))
                        pe.wait_ge(gate_sb, g.tiles(t))
                        for h in range(HEADS):
                            r, m = h % 4, h // 4
                            last = pe.matmul(A[:, r, m * P:(m + 1) * P], qkT[r * KD:(r + 1) * KD, HG + m, :],
                                             qkT[r * KD:(r + 1) * KD, m, :], start=True, stop=True,
                                             tile_position=(r * KD, 0))
                        last.then_inc(scores_ps, 1)
                    elif part == "OUT":
                        pe.wait_ge(scores_sb, g.tiles(t, 2))
                        if c:
                            pe.wait_ge(state_sb, g.states(c, HG))
                        for m in range(HG):
                            if c:
                                pe.matmul(A[:, 2 + m, 0:OW], qkT[:, m, :], state[:, m, :], start=True, stop=False,
                                          skip_group_check=True)
                            for r in range(4):
                                last = pe.matmul(A[:, 2 + m, r * HE:(r + 1) * HE], scores[:, r, m, :],
                                                 v[:, 4 * m + r, :], start=(c == 0 and r == 0), stop=(r == 3),
                                                 skip_group_check=True)
                        last.then_inc(out_ps, 1)
                        if c < CHUNKS - 1:
                            for m in range(HG):
                                last = pe.matmul(A[:, m, 0:OW], qk[:, t % 2, (HG + m) * P:(HG + m + 1) * P],
                                                 v[:, 4 * m:4 * m + 4, :].rearrange("p h e -> p (h e)"),
                                                 start=True, stop=True)
                            last.then_inc(state_ps, 1)
                    elif part == "YT":
                        pe.wait_ge(y_sb, g.tiles(t))
                        for k in range(VC):
                            last = pe.transpose(A[:, 3, k * P:(k + 1) * P], y[:, k * P:(k + 1) * P], ident)
                        last.then_inc(yT_ps, 1)
                    elif part == "WO":
                        pe.wait_ge(yT_high, g.tiles(t))
                        if g.first() and t == 0:
                            pe.wait_ge(w_low, FIRST_PARTS)
                        o = A[:, 2, 0:D]
                        for w in (wo_h, wo_l):
                            for k in range(VC):
                                pe.matmul(o, yT_h[:, k, :], w[:, k, :], start=(w is wo_h and k == 0), stop=False)
                        pe.wait_ge(yT_low, g.tiles(t))
                        for k in range(VC):
                            last = pe.matmul(o, yT_l[:, k, :], wo_h[:, k, :], start=False, stop=(k == VC - 1))
                        last.then_inc(wo_ps, 1)
                    elif part in ("H1", "H3"):
                        i, w = t, (w1 if part == "H1" else w3)
                        if part == "H1":
                            if i == 0:
                                pe.wait_ge(x1T_low, g.tiles(TPG - 1))
                                if g.first():
                                    pe.wait_ge(w_low, len(parts))
                            pe.wait_ge(act1_sb, g.experts(i - 1))
                        else:
                            pe.wait_ge(hid_sb, g.experts(i - 1))
                        pairs = [(w(wf, i, k), a[:, g.p, k, :]) for wf, a in ((wf_h, x1_h), (wf_l, x1_h), (wf_h, x1_l))
                                 for k in range(KC)]
                        split_product(F[:, 0 if part == "H1" else 1, :], pairs).then_inc(
                            h1_ps if part == "H1" else h3_ps, 1)
                    elif part == "W":
                        i = t
                        pe.wait_ge(hid_low, g.experts(i))
                        pe.wait_ge(sum_sb, g.experts(i - (2 if i == 1 else 1), 4))
                        for s in range(TPG):
                            cut = slice(s * P, (s + 1) * P)
                            pairs = [(a[:, e % 2, cut], w2(w, e)) for e in ((0, 1) if i == 1 else (i,))
                                     for a, w in ((hid_h, wf_h), (hid_h, wf_l), (hid_l, wf_h))]
                            last = split_product(F[:, 2 + s // 2, (s % 2) * D:(s % 2 + 1) * D], pairs)
                            if s % 2:
                                last.then_inc(ffn_ps, 2 if i == 1 else 1)

            for counter in (h1_ps, h3_ps, ffn_ps):
                pe.sem_inc(counter, START)
            pe.wait_ge(s_cst, 16)
            whole_run(pe, group)

        @block.scalar
        def _(act):
            def split_x(g, t):
                if t == 0:
                    act.wait_ge(s_xT, g.groups(16))
                if positive(g.tiles(t - 2)):
                    act.wait_ge(g_proj, g.tiles(t - 2))
                act.activation(x_h[:, t % 2, :, :], xraw[:, :, t * P:(t + 1) * P], ACT.Copy).then_inc(x_high, 1)

            def next_x(g, t):
                if t < TPG - 1:
                    split_x(g, t + 1)
                elif not (isinstance(g.b, int) and g.index() == NG - 1):
                    split_x(Group(g.b, g.at + 1), 0)

            def weight(n):
                _, width, high, _ = parts[n]
                act.wait_ge(s_stage[n % 2], 16 * (n // 2 + 1))
                act.activation(high, stage[n % 2][:, 0:width], ACT.Copy).then_inc(w_high, 1)

            def group(ga, gf):
                for part, t, g in parts_of(ga, gf):
                    if part == "V":
                        act.wait_ge(v_proj, g.tiles(t))
                        act.activation(v[:, :, 0:HD], A[:, 1, :].rearrange("p (h e) -> p h e", h=HEADS),
                                       ACT.Copy).then_inc(v_sb, 1)
                    elif part == "X1T":
                        act.wait_ge(x1T_ps, g.tiles(t))
                        src = A[:, 3, 0:D].rearrange("p (k n) -> p k n", k=KC)
                        act.activation(x1T[:, :, :], src, ACT.Copy).then_inc(x1T_sb, 1)
                        if t == 0 and positive(g.before(2).experts(NE - 1)):
                            act.wait_ge(h3_ps, g.before(2).experts(NE - 1))
                        act.activation(x1_h[:, g.p, :, t * P:(t + 1) * P], src, ACT.Copy).then_inc(x1T_high, 1)
                    elif part == "G":
                        act.wait_ge(g_proj, g.tiles(t))
                        if positive(g.tiles(t - 1)):
                            act.wait_ge(gated_sb, g.tiles(t - 1, HG))
                        act.activation(gate[:, :], A[:, 2, :], ACT.Silu).then_inc(gate_sb, 1)
                    elif part == "LOGITS" and t == TPG - 1:
                        act.wait_ge(offset_sb, g.groups())
                        act.activation(share[:, :, :], offset[:, :, :], ACT.Tanh).then_inc(share_sb, 1)
                    elif part == "QKT":
                        act.wait_ge(qkT_ps, g.tiles(t))
                        if positive(g.tiles(t - 1)):
                            act.wait_ge(out_ps, g.tiles(t - 1))
                        act.activation(qkT[:, :, :], A[:, 3, :].rearrange("p (k n) -> p k n", k=4),
                                       ACT.Copy).then_inc(qkT_sb, 1)
                        next_x(g, t)
                    elif part == "OUT":
                        act.wait_ge(out_ps, g.tiles(t))
                        if positive(g.tiles(t - 1)):
                            act.wait_ge(meansq_sb, g.tiles(t - 1))
                        act.activation(squares[:, :, :].rearrange("p (m r) e -> p m (r e)", m=HG), A[:, 2:4, 0:OW],
                                       ACT.Square, scale=float(HD) ** -0.5).then_inc(sq_sb, 1)
                    elif part == "YT":
                        act.wait_ge(yT_ps, g.tiles(t))
                        act.activation(yT_h[:, :, :], A[:, 3, :].rearrange("p (k n) -> p k n", k=VC),
                                       ACT.Copy).then_inc(yT_high, 1)
                    elif part == "WO" and gf is None:
                        for n in range(FIRST_PARTS + 3 * t, min(FIRST_PARTS + 3 * t + 3, len(parts))):
                            weight(n)
                    elif part == "H1":
                        act.wait_ge(h1_ps, g.experts(t))
                        act.wait_ge(hid_sb, g.experts(t - 1))
                        act.activation(act1[:, :], F[:, 0, :], ACT.Silu).then_inc(act1_sb, 1)
                    elif part == "H3":
                        act.wait_ge(hid_sb, g.experts(t))
                        act.wait_ge(ffn_ps, g.down(t - 2))
                        act.activation(hid_h[:, t % 2, :], hid[:, t % 2, :], ACT.Copy).then_inc(hid_high, 1)

            for counter in (act1_sb, hid_high):
                act.sem_inc(counter, START)
            weight(0)
            split_x(Group(0, 0), 0)
            for n in range(1, FIRST_PARTS):
                weight(n)
            whole_run(act, group)

        @block.gpsimd
        def _(pool):
            def split_x(g, t):
                pool.wait_ge(x_high, g.tiles(t))
                if positive(g.tiles(t - 2)):
                    pool.wait_ge(g_proj, g.tiles(t - 2))
                pool.tensor_tensor(x_l[:, t % 2, :, :], xraw[:, :, t * P:(t + 1) * P],
                                   x_h[:, t % 2, :, :].bitcast(f32), ALU.subtract).then_inc(x_low, 1)

            def next_x(g, t):
                if t < TPG - 1:
                    split_x(g, t + 1)
                elif not (isinstance(g.b, int) and g.index() == NG - 1):
                    split_x(Group(g.b, g.at + 1), 0)

            def group(ga, gf):
                for part, t, g in parts_of(ga, gf):
                    c = TPG * g.p + t
                    if part == "QK":
                        pool.wait_ge(qk_scaled, g.tiles(t))
                        if positive(g.tiles(t - 1)):
                            pool.wait_ge(qk_rot, g.tiles(t - 1))
                        src = qk_s[:, :].rearrange("p (h k) -> p h k", k=KD)
                        dst = qk_w[:, :].rearrange("p (h k) -> p h k", k=KD)
                        half = KD // 2
                        for lo, hi in ((0, half), (half, KD)):
                            s = sin[:, c:c + 1, lo:hi].to_broadcast([P, 2 * HEADS, half])
                            pool.tensor_tensor(dst[:, :, lo:hi], src[:, :, half - lo:KD - lo], s,
                                               ALU.mult).then_inc(qk_sin, 1)
                    elif part == "QKT":
                        next_x(g, t)
                    elif part == "OUT":
                        pool.wait_ge(meansq_sb, g.tiles(t))
                        if positive(g.tiles(t - 1)):
                            pool.wait_ge(y_sb, g.tiles(t - 1))
                        pool.tensor_tensor(rms[:, :], meansq[:, :], minus_half[:, :], ALU.pow).then_inc(rms_sb, 1)
                    elif part == "WO":
                        pool.wait_ge(var_sb, g.tiles(t))
                        if positive(g.tiles(t - 1)):
                            pool.wait_ge(x1_sb, g.tiles(t - 1))
                        pool.tensor_tensor(rstd[:, :], var_eps[:, :], minus_half[:, 0:1], ALU.pow).then_inc(rstd_sb, 1)
                    elif part == "H3":
                        pool.wait_ge(hid_high, g.experts(t))
                        pool.wait_ge(ffn_ps, g.down(t - 2))
                        pool.tensor_tensor(hid_l[:, t % 2, :], hid[:, t % 2, :], hid_h[:, t % 2, :].bitcast(f32),
                                           ALU.subtract).then_inc(hid_low, 1)
                    elif part == "W" and t == NE - 1:
                        pool.wait_ge(var2_sb, g.groups())
                        pool.tensor_tensor(rstd2[:, :], var_eps2[:, :], minus_half[:, 0:TPG], ALU.pow)\
                            .then_inc(rstd2_sb, 1)

            pool.sem_inc(hid_low, START)
            pool.memset(minus_half[:, :], -0.5).then_inc(ready0, 1)
            pool.memset(v[:, :, HD:HE], 1.0).then_inc(ready0, 1)
            pool.memset(logits[:, :, EXPERTS:], PAD).then_inc(ready0, 1)
            pool.memset(top2[:, :, 2:8], PAD).then_inc(ready0, 1)
            pool.wait_ge(ready0, 4)
            pool.wait_ge(s_cst, 16)
            split_x(Group(0, 0), 0)
            whole_run(pool, group)

        @block.vector
        def _(dve):
            def weight(n):
                _, width, high, low = parts[n]
                dve.wait_ge(w_high, n + 1)
                dve.tensor_tensor(low, stage[n % 2][:, 0:width], high.bitcast(f32), ALU.subtract).then_inc(w_low, 1)

            def group(ga, gf):
                for part, t, g in parts_of(ga, gf):
                    c = TPG * g.p + t
                    if part == "QK":
                        dve.wait_ge(qk_proj, g.tiles(t))
                        if positive(g.tiles(t - 1)):
                            dve.wait_ge(qk_sin, g.tiles(t - 1, 2))
                        heads = lambda a: a.rearrange("p (h k) -> p h k", k=KD)
                        dve.tensor_tensor(heads(qk_s[:, :]), heads(A[:, 0, :]),
                                          gamma.unsqueeze(2).to_broadcast([P, 2 * HEADS, KD]),
                                          ALU.mult).then_inc(qk_scaled, 1)
                        dve.wait_ge(qk_scaled, g.tiles(t))
                        dve.tensor_tensor(heads(qk_c[:, :]), heads(qk_s[:, :]),
                                          cos[:, c:c + 1, :].to_broadcast([P, 2 * HEADS, KD]),
                                          ALU.mult).then_inc(qk_cos, 1)
                    elif part == "V":
                        dve.wait_ge(qk_cos, g.tiles(t))
                        dve.wait_ge(qk_sin, g.tiles(t, 2))
                        dve.tensor_tensor(qk[:, t % 2, :], qk_c[:, :], qk_w[:, :], ALU.add).then_inc(qk_rot, 1)
                    elif part == "X1T":
                        dve.wait_ge(x1T_high, g.tiles(t))
                        cut = slice(t * P, (t + 1) * P)
                        dve.tensor_tensor(x1_l[:, g.p, :, cut], A[:, 3, 0:D].rearrange("p (k n) -> p k n", k=KC),
                                          x1_h[:, g.p, :, cut].bitcast(f32), ALU.subtract).then_inc(x1T_low, 1)
                    elif part == "LOGITS":
                        dve.wait_ge(logits_ps, g.tiles(t))
                        dve.tensor_tensor(logits[:, t, 0:EXPERTS], A[:, 0, 0:EXPERTS], br[:, :],
                                          ALU.add).then_inc(logits_sb, 1)
                        if t == TPG - 1:
                            route(g)
                    elif part == "SCORES":
                        dve.wait_ge(scores_ps, g.tiles(t))
                        for m in range(2):
                            dve.tensor_tensor(
                                scores[:, 2 * m:2 * m + 2, :, :].rearrange("p b m n -> p (b m) n"),
                                A[:, 2 * m:2 * m + 2, 0:2 * P].rearrange("p b (m n) -> p b m n", m=2),
                                causal.unsqueeze(1).to_broadcast([P, 4, P]), ALU.mult).then_inc(scores_sb, 1)
                    elif part == "OUT":
                        retention_out(g, t, c)
                    elif part == "YT":
                        dve.wait_ge(yT_high, g.tiles(t))
                        dve.tensor_tensor(yT_l[:, :, :], A[:, 3, :].rearrange("p (k n) -> p k n", k=VC),
                                          yT_h[:, :, :].bitcast(f32), ALU.subtract).then_inc(yT_low, 1)
                    elif part == "WO":
                        layer_norm(g, t)
                        if gf is None:
                            for n in range(FIRST_PARTS + 3 * t, min(FIRST_PARTS + 3 * t + 3, len(parts))):
                                weight(n)
                    elif part == "H3":
                        dve.wait_ge(act1_sb, g.experts(t))
                        dve.wait_ge(h3_ps, g.experts(t))
                        dve.wait_ge(hid_low, g.experts(max(t - 2, -1)))
                        dve.tensor_tensor(hid[:, t % 2, :], F[:, 1, :], act1[:, :], ALU.mult).then_inc(hid_sb, 1)
                    elif part == "W":
                        add_expert(g, t)
                        if t == NE - 1:
                            layer_norm_out(g)

            def hold():
                dve.sem_inc(held, 1)

            def retention_out(g, t, c):
                four = lambda a: a.rearrange("p (r e) -> p r e", e=HE)
                dve.wait_ge(sq_sb, g.tiles(t))
                dve.tensor_reduce(sumsq[:, :], squares[:, :, 0:HD], AX.X, ALU.add).then_inc(norm_step, 1)
                dve.tensor_tensor(denom[:, :], squares[:, :, HD], rowsum[:, c, :], ALU.max).then_inc(norm_step, 1)
                dve.wait_ge(norm_step, g.tiles(t, 2))
                dve.scalar_tensor_tensor(meansq[:, :], denom[:, :], HD * EPS, sumsq[:, :], ALU.mult,
                                         ALU.add).then_inc(meansq_sb, 1)
                dve.wait_ge(gate_sb, g.tiles(t))
                for m in range(HG):
                    dve.tensor_tensor(gated[:, m * 4 * HD:(m + 1) * 4 * HD].rearrange("p (r e) -> p r e", e=HD),
                                      four(A[:, 2 + m, 0:OW])[:, :, 0:HD],
                                      gate[:, m * 4 * HD:(m + 1) * 4 * HD].rearrange("p (r e) -> p r e", e=HD),
                                      ALU.mult).then_inc(gated_sb, 1)
                if c < CHUNKS - 1:
                    dve.wait_ge(state_ps, g.states(c + 1))
                    if c == 0:
                        dve.tensor_tensor(state[:, :, :], A[:, 0:2, 0:OW], block_decay, ALU.mult)\
                            .then_inc(state_sb, HG)
                    else:
                        dve.tensor_tensor(state_new[:, :, :], A[:, 0:2, 0:OW], block_decay, ALU.mult)\
                            .then_inc(state_upd, 1)
                        dve.wait_ge(state_upd, g.states(c, 1, CHUNKS - 2))
                        for m in range(HG):
                            dve.scalar_tensor_tensor(state[:, m, :], state[:, m, :], gamma_chunk[:, m:m + 1],
                                                     state_new[:, m, :], ALU.mult, ALU.add).then_inc(state_sb, 1)
                dve.wait_ge(rms_sb, g.tiles(t))
                dve.wait_ge(gated_sb, g.tiles(t, HG))
                dve.tensor_tensor(y[:, :].rearrange("p (h e) -> p h e", e=HD),
                                  gated[:, :].rearrange("p (h e) -> p h e", e=HD),
                                  rms[:, :].unsqueeze(2).to_broadcast([P, HEADS, HD]), ALU.mult).then_inc(y_sb, 1)

            def layer_norm(g, t):
                dve.wait_ge(wo_ps, g.tiles(t))
                if t == 0:
                    dve.wait_ge(s_x[g.p], g.rows(16))
                dve.tensor_tensor(res[:, :], A[:, 2, 0:D], xres[:, g.p, t, :], ALU.add).then_inc(ln_step, 1)
                dve.wait_ge(ln_step, g.tiles(t, 3) - 2)
                dve.bn_stats(stats[:, :], res[:, :]).then_inc(ln_step, 1)
                dve.wait_ge(ln_step, g.tiles(t, 3) - 1)
                hold()
                dve.bn_aggr(moments[:, :], stats[:, :]).then_inc(ln_step, 1)
                dve.wait_ge(ln_step, g.tiles(t, 3))
                dve.tensor_scalar(var_eps[:, :], moments[:, 1:2], EPS, None, ALU.add).then_inc(var_sb, 1)
                dve.wait_ge(rstd_sb, g.tiles(t))
                if t == 0 and not g.first():
                    dve.wait_ge(s_out, g.groups(16, -1) + START)
                dve.tensor_scalar(x1[:, g.p, t, :], res[:, :], moments[:, 0:1], rstd[:, :], ALU.subtract,
                                  ALU.mult).then_inc(x1_sb, 1)

            def route(g):
                n = lambda k: g.groups(2 * TPG + 6, 0) + k
                dve.wait_ge(logits_sb, g.tiles(TPG - 1))
                hold()
                for s in range(TPG):
                    dve.max(top8[:, s, :], logits[:, s, 0:EXPERTS]).then_inc(route_step, 1)
                dve.wait_ge(route_step, n(TPG))
                dve.tensor_copy(top2[:, :, 0:2], top8[:, :, 0:2]).then_inc(route_step, 1)
                dve.tensor_tensor(middle[:, :], top8[:, :, 0], top8[:, :, 1], ALU.add).then_inc(route_step, 1)
                dve.wait_ge(route_step, n(TPG + 2))
                dve.scalar_tensor_tensor(offset[:, :, :], middle[:, :].unsqueeze(2).to_broadcast([P, TPG, EXPERTS]),
                                         -0.5, logits[:, :, 0:EXPERTS], ALU.mult, ALU.add).then_inc(offset_sb, 1)
                for s in range(TPG):
                    dve.match_replace(without[:, s, :], top2[:, s, :], logits[:, s, :], -PAD).then_inc(route_step, 1)
                dve.wait_ge(route_step, n(2 * TPG + 2))
                dve.tensor_tensor(chosen[:, :, :], logits[:, :, 0:EXPERTS], without[:, :, 0:EXPERTS],
                                  ALU.not_equal).then_inc(route_step, 1)
                dve.wait_ge(share_sb, g.groups())
                dve.tensor_scalar(half_share[:, :, :], share[:, :, :], 0.5, 0.5, ALU.mult, ALU.add)\
                    .then_inc(route_step, 1)
                dve.wait_ge(route_step, n(2 * TPG + 4))
                dve.tensor_tensor(gates[:, g.p, :, :], half_share[:, :, :], chosen[:, :, :], ALU.mult)\
                    .then_inc(route_step, 2)

            def add_expert(g, i):
                if i == 1:
                    for m in range(2):
                        dve.wait_ge(ffn_ps, g.experts(1, 2) - 2 * (1 - m))
                        acc = x1[:, g.p, 2 * m:2 * m + 2, :].rearrange("p t d -> p (t d)")
                        dve.tensor_tensor(acc, F[:, 2 + m, :], acc, ALU.add).then_inc(sum_sb, 4)
                    return
                if i == 2:
                    dve.wait_ge(route_step, g.groups(2 * TPG + 6))
                for s in range(TPG):
                    if s % 2 == 0:
                        dve.wait_ge(ffn_ps, g.experts(i, 2) - 1 + s // 2)
                    dve.wait_ge(sum_sb, g.experts(i - 1, 4) if i == 2 else g.experts(i - 1, 4) + s + 1 - TPG)
                    dve.scalar_tensor_tensor(x1[:, g.p, s, :], F[:, 2 + s // 2, (s % 2) * D:(s % 2 + 1) * D],
                                             gates[:, g.p, s, i - SHARED:i - SHARED + 1], x1[:, g.p, s, :],
                                             ALU.mult, ALU.add).then_inc(sum_sb, 1)

            def layer_norm_out(g):
                for s in range(TPG):
                    dve.wait_ge(sum_sb, g.experts(NE - 1, 4) + s + 1 - TPG)
                    dve.bn_stats(stats2[:, s, :], x1[:, g.p, s, :]).then_inc(ln2_step, 1)
                for s in range(TPG):
                    dve.wait_ge(ln2_step, g.groups(2 * TPG, 0) + s + 1)
                    hold()
                    dve.bn_aggr(moments2[:, s, :], stats2[:, s, :]).then_inc(ln2_step, 1)
                dve.wait_ge(ln2_step, g.groups(2 * TPG))
                dve.tensor_scalar(var_eps2[:, :], moments2[:, :, 1], EPS, None, ALU.add).then_inc(var2_sb, 1)
                dve.wait_ge(rstd2_sb, g.groups())
                for s in range(TPG):
                    dve.tensor_scalar(x1[:, g.p, s, :], x1[:, g.p, s, :], moments2[:, s, 0:1], rstd2[:, s:s + 1],
                                      ALU.subtract, ALU.mult).then_inc(result_sb, 1)

            for counter in (hid_sb, sum_sb):
                dve.sem_inc(counter, START)
            for n in range(FIRST_PARTS):
                weight(n)
            dve.wait_ge(ready0, 4)
            dve.wait_ge(s_cst, 16)
            dve.wait_ge(s_router, 32)
            whole_run(dve, group)


def shape_constants():
    f = np.float32
    lin = np.linspace(0.0, 1.0, KD // 2).astype(f)
    angle = (f(1.0) / np.power(f(10000.0), lin)).astype(f)
    pos = np.arange(SEQ, dtype=f)
    arg = (pos[:, None] * angle[None, :]).astype(f).astype(np.float64)
    s, c = np.sin(arg), np.cos(arg)
    decay = np.log1p(-2.0 ** (-5.0 - np.arange(HEADS, dtype=np.float64)))
    i = np.arange(P, dtype=np.float64)
    t = {}
    grow = np.exp(i[:, None] * decay[None, :])
    t["gamma"] = np.concatenate([grow, float(KD) ** -0.5 / grow], 1)
    by_chunk = lambda a: a.reshape(CHUNKS, P, -1).transpose(1, 0, 2).reshape(P, -1)
    t["cos"] = by_chunk(np.concatenate([c, c], 1))
    t["sin"] = by_chunk(np.concatenate([-s, s], 1))
    t["causal"] = (i[:, None] <= i[None, :]).astype(np.float64)
    block = np.zeros((P, HG, OW))
    per_chunk = np.exp(P * decay)
    for h in range(HEADS):
        m, r = h // 4, h % 4
        block[r * KD:(r + 1) * KD, m, r * HE:(r + 1) * HE] = per_chunk[h]
    t["block"] = block.reshape(P, -1)
    t["gamma_chunk"] = np.repeat(per_chunk.reshape(HG, 4).T, KD, axis=0)
    rows = np.cumsum(np.exp(np.arange(SEQ)[:, None] * decay[None, :]), 0)
    t["rowsum"] = by_chunk(rows / HD)
    t["ident"] = np.eye(P)
    return np.concatenate([t[name].reshape(P, width) for name, width in CONST_WIDTHS], 1).astype(f)


def kernel(**inputs):
    import numpy as _np
    import concourse.bacc as _bacc
    from concourse import mybir as _mybir
    from concourse.bass_utils import run_bass_kernel_spmd as _run

    a = {k.removeprefix("L0_"): _np.asarray(v) for k, v in inputs.items()}
    x = a["attn_x"].reshape(BATCH * SEQ, D)
    even_odd = _np.arange(D).reshape(HEADS, KD // 2, 2).transpose(0, 2, 1).reshape(-1)
    rows = lambda w: w.reshape(-1, P, w.shape[-1]).transpose(1, 0, 2)
    flat = lambda w: rows(w).reshape(P, -1)
    qk = _np.concatenate([a["attn_wq"][:, even_odd], a["attn_wk"][:, even_odd]], 1)
    experts = [(a["ffn_shared_w1"][e], a["ffn_shared_w3"][e], a["ffn_shared_w2"][e]) for e in range(SHARED)]
    experts += [(a["ffn_routed_w1"][e], a["ffn_routed_w3"][e], a["ffn_routed_w2"][e]) for e in range(EXPERTS)]
    arrays = {
        "x": x,
        "xT": x.reshape(NG, GT, KC, P).transpose(0, 3, 2, 1),
        "w_att": _np.stack([flat(w) for w in (qk, a["attn_wv"], a["attn_wg"])]),
        "w_wo": flat(a["attn_wo"]),
        "w_ffn": _np.stack([_np.concatenate([flat(m) for m in e], 1) for e in experts]),
        "w_router": rows(a["ffn_router_w"]),
        "b_router": _np.repeat(a["ffn_router_b"][None, :], P, 0),
        "consts": shape_constants(),
    }
    arrays = {k: _np.ascontiguousarray(v) for k, v in arrays.items()}

    nc = _bacc.Bacc("TRN2", target_bir_lowering=False, num_devices=1)
    args = [nc.dram_tensor(k, v.shape, _mybir.dt.from_np(v.dtype), kind="ExternalInput").ap()
            for k, v in arrays.items()]
    out = nc.dram_tensor("out", (BATCH * SEQ, D), _mybir.dt.float32, kind="ExternalOutput").ap()
    retention_moe_kernel(nc, *args, out)
    r = _run(nc, [arrays], core_ids=[0])
    return r.results[0]["out"].reshape(BATCH, SEQ, D)
```

```python
import math
from contextlib import ExitStack

import numpy as np

import concourse.bass as bass
from concourse import mybir

BATCH, SEQ, D = 8, 1024, 256
HEADS, KD, HD = 8, 32, 64
VD = HEADS * HD
EXPERTS, SHARED, HID = 8, 2, 128
EPS = 1e-5

P = 128
TPG = 4
GPB = SEQ // (P * TPG)
CHUNKS = SEQ // P
NG = BATCH * GPB
GT = TPG * P
KC = D // P
VC = VD // P
HG = HEADS // 4
HE = HD + 1
OW = 4 * HE
NE = SHARED + EXPERTS
EW = KC * HID * 2 + D
PROJ = 3
PAD = 3.0e38

CONST_WIDTHS = [("gamma", 2 * HEADS), ("cos", CHUNKS * KD), ("sin", CHUNKS * KD), ("causal", P),
                ("block", HG * OW), ("gamma_chunk", HG), ("rowsum", CHUNKS * HEADS), ("ident", P)]
CONST_AT, _at = {}, 0
for _name, _width in CONST_WIDTHS:
    CONST_AT[_name] = (_at, _at + _width)
    _at += _width
CONSTS = _at

LATE = ("NORM", "YT", "WO", "X1", "X1T", "LOGITS")
SLOTS = [s.split() for s in (
    "NORM QK V YT G WO F QKT X1 F X1T F LOGITS F SCORES F OUT F F",
    "NORM QK F V YT G WO F QKT X1 X1T F LOGITS F SCORES F OUT F F",
    "NORM QK V YT G F WO QKT X1 F X1T F LOGITS F SCORES F OUT F F F",
    "NORM QK V YT G WO F QKT X1 F X1T F LOGITS F SCORES F OUT F F",
)]
PLACES = {"scalar": {"V": 1.5, "X1T": 0.5, "QKT": 1}, "vector": {"SUM1": 0, "SUM2": 0}, "gpsimd": {}}


def last_steps(g):
    return [("H1", NE - 1, g), ("W", NE - 3, g), ("H3", NE - 1, g), ("W", NE - 2, g), ("W", NE - 1, g)]


def feed_forward_steps(g):
    steps = [(part, i, g) for part, i in (("H1", 0), ("H3", 0), ("H1", 1), ("H3", 1), ("H1", 2), ("W", 1), ("H3", 2))]
    for i in range(3, NE - 1):
        steps += [("H1", i, g), ("H3", i, g)] + ([("W", i - 1, g)] if i < NE - 2 else [])
    return steps


def schedule(ga, gf):
    out = []
    if not ga:
        for n, step in enumerate(last_steps(gf.before(1))):
            out += [step] + ([(LATE[n], TPG - 1, gf)] if n < 3 else [])
        out += [(part, TPG - 1, gf) for part in LATE[3:]] + [("RESULT", 0, gf.before(1))]
        return out + feed_forward_steps(gf) + last_steps(gf) + [("RESULT", 0, gf)]
    steps = []
    if gf:
        steps = [step if gf.before(1).exists() else None for step in last_steps(gf.before(1))]
        steps += feed_forward_steps(gf)
    for t in range(TPG):
        for part in SLOTS[t]:
            if part == "F":
                step = steps.pop(0) if steps else None
                if step:
                    out.append(step)
            elif part in LATE:
                if t:
                    out.append((part, t - 1, ga))
                elif gf:
                    out.append((part, TPG - 1, gf))
            else:
                out.append((part, t, ga))
                if part == "OUT" and t == 0 and gf and gf.before(1).exists():
                    out.append(("RESULT", 0, gf.before(1)))
    return out + steps


def schedule_of(engine, ga, gf):
    parts = []
    for n, (part, t, g) in enumerate(schedule(ga, gf)):
        halves = ("SUM1", "SUM2") if (engine, part) == ("vector", "W") else (part,)
        parts += [(n + PLACES[engine].get(p, 0), len(parts), (p, t, g)) for p in halves]
    return [p for _, _, p in sorted(parts, key=lambda x: x[:2])]


class Group:

    def __init__(self, b, at):
        self.b, self.at = b, at
        self.p = at % GPB

    def tiles(self, t, per=1):
        return self.b * (per * CHUNKS) + per * (TPG * self.at + t + 1)

    def experts(self, i, per=1):
        return self.b * (per * NE * GPB) + per * (NE * self.at + i + 1)

    def down(self, i):
        return self.experts(max(i, -1) or 1, 2)

    def groups(self, per=1, k=1):
        return self.b * (per * GPB) + per * (self.at + k)

    def rows(self, per):
        return self.b * per + per * (self.at // GPB + 1)

    def states(self, chunk, per=1, updates=CHUNKS - 1):
        return self.b * (per * updates) + per * (self.at // GPB * updates + chunk)

    def index(self):
        return self.b * GPB + self.at

    def first(self):
        return isinstance(self.b, int) and self.index() == 0

    def exists(self):
        return not isinstance(self.b, int) or self.index() >= 0

    def before(self, k):
        return Group(self.b, self.at - k)


def positive(value):
    return not isinstance(value, int) or value > 0


def retention_moe_kernel(nc, x, xT, w_att, w_wo, w_ffn, w_router, b_router, consts, out):
    f32, f32r = mybir.dt.float32, mybir.dt.float32r
    ALU, ACT, AX = mybir.AluOpType, mybir.ActivationFunctionType, mybir.AxisListType

    x_v = x.rearrange("(g t p) d -> g p t d", t=TPG, p=P)
    out_v = out.rearrange("(g t p) d -> g p t d", t=TPG, p=P)

    with ExitStack() as ctx:
        def sb(name, shape, dt=f32):
            return ctx.enter_context(nc.sbuf_tensor(name, shape, dt))

        def sem(name):
            return ctx.enter_context(nc.semaphore(name))

        watt_h, watt_l = sb("watt_h", [P, PROJ, KC, 512], f32r), sb("watt_l", [P, PROJ, KC, 512], f32r)
        wo_h, wo_l = sb("wo_h", [P, VC, D], f32r), sb("wo_l", [P, VC, D], f32r)
        wf_h, wf_l = sb("wf_h", [P, NE, EW], f32r), sb("wf_l", [P, NE, EW], f32r)
        wr = sb("wr", [P, KC, EXPERTS])
        br = sb("br", [P, EXPERTS])
        cst = sb("cst", [P, CONSTS])

        def const(name):
            return cst[:, CONST_AT[name][0]:CONST_AT[name][1]]

        gamma = const("gamma")
        cos = const("cos").rearrange("p (c k) -> p c k", c=CHUNKS)
        sin = const("sin").rearrange("p (c k) -> p c k", c=CHUNKS)
        causal = const("causal")
        block_decay = const("block").rearrange("p (g w) -> p g w", g=HG)
        gamma_chunk = const("gamma_chunk")
        rowsum = const("rowsum").rearrange("p (c h) -> p c h", c=CHUNKS)
        ident = const("ident")

        xraw = sb("xraw", [P, KC, GT])
        x_h, x_l = sb("x_h", [P, 2, KC, P], f32r), sb("x_l", [P, 2, KC, P], f32r)
        xres = sb("xres", [P, 2, TPG, D])
        qk_s, qk_c, qk_w = sb("qk_s", [P, 512]), sb("qk_c", [P, 512]), sb("qk_w", [P, 512])
        qk = sb("qk", [P, 2, 512])
        qkT = sb("qkT", [P, 4, P])
        v = sb("v", [P, HEADS, HE])
        gate = sb("gate", [P, VD])
        scores = sb("scores", [P, 4, 2, P])
        state = sb("state", [P, HG, OW])
        state_new = sb("state_new", [P, HG, OW])
        squares = sb("squares", [P, HEADS, HE])
        sumsq, denom = sb("sumsq", [P, HEADS]), sb("denom", [P, HEADS])
        meansq, rms = sb("meansq", [P, HEADS]), sb("rms", [P, HEADS])
        minus_half = sb("minus_half", [P, HEADS])
        gated, y = sb("gated", [P, VD]), sb("y", [P, VD])
        yT_h, yT_l = sb("yT_h", [P, VC, P], f32r), sb("yT_l", [P, VC, P], f32r)
        res = sb("res", [P, D])
        stats, moments = sb("stats", [P, 6]), sb("moments", [P, 2])
        var_eps, rstd = sb("var_eps", [P, 1]), sb("rstd", [P, 1])
        x1 = sb("x1", [P, 2, TPG, D])
        x1T = sb("x1T", [P, KC, P])
        x1_h, x1_l = sb("x1_h", [P, 2, KC, GT], f32r), sb("x1_l", [P, 2, KC, GT], f32r)
        logits = sb("logits", [P, TPG, EXPERTS + 6])
        top8, top2 = sb("top8", [P, TPG, 8]), sb("top2", [P, TPG, 8])
        without = sb("without", [P, TPG, EXPERTS + 6])
        middle, offset = sb("middle", [P, TPG]), sb("offset", [P, TPG, EXPERTS])
        chosen, share = sb("chosen", [P, TPG, EXPERTS]), sb("share", [P, TPG, EXPERTS])
        half_share = sb("half_share", [P, TPG, EXPERTS])
        gates = sb("gates", [P, 2, TPG, EXPERTS])
        act1 = sb("act1", [P, GT])
        hid = sb("hid", [P, 2, GT])
        hid_h, hid_l = sb("hid_h", [P, 2, GT], f32r), sb("hid_l", [P, 2, GT], f32r)
        stats2, moments2 = sb("stats2", [P, TPG, 6]), sb("moments2", [P, TPG, 2])
        var_eps2, rstd2 = sb("var_eps2", [P, TPG]), sb("rstd2", [P, TPG])

        A = ctx.enter_context(nc.psum_tensor("A", [P, 4, 512], f32))
        F = ctx.enter_context(nc.psum_tensor("F", [P, 4, 512], f32))

        s_cst, s_router, s_out = sem("s_cst"), sem("s_router"), sem("s_out")
        s_stage = [sem("s_stage0"), sem("s_stage1")]
        s_xT, s_x = sem("s_xT"), [sem("s_x0"), sem("s_x1")]
        w_high, w_low = sem("w_high"), sem("w_low")
        ready0 = sem("ready0")
        x_high, x_low = sem("x_high"), sem("x_low")
        qk_proj, v_proj, g_proj = sem("qk_proj"), sem("v_proj"), sem("g_proj")
        qk_scaled, qk_cos, qk_sin, qk_rot = sem("qk_scaled"), sem("qk_cos"), sem("qk_sin"), sem("qk_rot")
        v_sb, gate_sb = sem("v_sb"), sem("gate_sb")
        qkT_ps, qkT_sb = sem("qkT_ps"), sem("qkT_sb")
        scores_ps, scores_sb = sem("scores_ps"), sem("scores_sb")
        out_ps, state_ps, state_upd, state_sb = sem("out_ps"), sem("state_ps"), sem("state_upd"), sem("state_sb")
        sq_sb, norm_step, meansq_sb, rms_sb = sem("sq_sb"), sem("norm_step"), sem("meansq_sb"), sem("rms_sb")
        gated_sb, y_sb = sem("gated_sb"), sem("y_sb")
        yT_ps, yT_high, yT_low = sem("yT_ps"), sem("yT_high"), sem("yT_low")
        wo_ps, ln_step, var_sb, rstd_sb, x1_sb = sem("wo_ps"), sem("ln_step"), sem("var_sb"), sem("rstd_sb"), sem("x1_sb")
        held = sem("held")
        x1T_ps, x1T_sb, x1T_high, x1T_low = sem("x1T_ps"), sem("x1T_sb"), sem("x1T_high"), sem("x1T_low")
        logits_ps, logits_sb = sem("logits_ps"), sem("logits_sb")
        route_step, offset_sb, share_sb = sem("route_step"), sem("offset_sb"), sem("share_sb")
        h1_ps, h3_ps, act1_sb, hid_sb, hid_high, hid_low = (sem("h1_ps"), sem("h3_ps"), sem("act1_sb"), sem("hid_sb"),
                                                            sem("hid_high"), sem("hid_low"))
        ffn_ps, sum_sb = sem("ffn_ps"), sem("sum_sb")
        ln2_step, var2_sb, rstd2_sb, result_sb = sem("ln2_step"), sem("var2_sb"), sem("rstd2_sb"), sem("result_sb")

        stage = [x1[:, 1, :, :].rearrange("p t d -> p (t d)"), xres[:, 1, :, :].rearrange("p t d -> p (t d)")]
        parts = []
        for j in range(PROJ):
            parts.append((w_att[j], KC * 512, watt_h[:, j, :, :].rearrange("p k n -> p (k n)"),
                          watt_l[:, j, :, :].rearrange("p k n -> p (k n)")))
        parts.append((w_wo, VC * D, wo_h[:, :, :].rearrange("p k n -> p (k n)"),
                      wo_l[:, :, :].rearrange("p k n -> p (k n)")))
        for i in range(NE):
            parts.append((w_ffn[i], EW, wf_h[:, i, :], wf_l[:, i, :]))
        FIRST_PARTS = PROJ + 1

        def w1(w, i, k):
            return w[:, i, k * HID:(k + 1) * HID]

        def w3(w, i, k):
            return w[:, i, (KC + k) * HID:(KC + k + 1) * HID]

        def w2(w, i):
            return w[:, i, 2 * KC * HID:EW]

        def whole_run(eng, group):
            group(Group(0, 0), None)
            group(Group(0, 1), Group(0, 0))
            with eng.Fori(1, BATCH) as b:
                group(Group(b, 0), Group(b, -1))
                group(Group(b, 1), Group(b, 0))
            group(None, Group(BATCH - 1, 1))

        block = ctx.enter_context(nc.Block())

        @block.sync
        def _(sp):
            def load_xT(g):
                if not g.first():
                    sp.wait_ge(x_low, g.before(1).tiles(TPG - 1))
                sp.dma_start(xraw[:, :, :], xT[g.index()]).then_inc(s_xT, 16)

            def load_x(g):
                if positive(g.groups(1, -1)):
                    sp.wait_ge(ln_step, g.before(2).tiles(TPG - 1, 3))
                sp.dma_start(xres[:, g.p, :, :], x_v[g.index()]).then_inc(s_x[g.p], 16)

            def store(g):
                sp.wait_ge(result_sb, g.groups(TPG))
                sp.dma_start(out_v[g.index()], x1[:, g.p, :, :]).then_inc(s_out, 16)

            for n, (src, width, _, _) in enumerate(parts):
                if n == 1:
                    load_xT(Group(0, 0))
                    sp.dma_start(cst[:, :], consts).then_inc(s_cst, 16)
                if n == FIRST_PARTS:
                    load_x(Group(0, 0))
                    sp.dma_start(wr[:, :, :], w_router).then_inc(s_router, 16)
                    sp.dma_start(br[:, :], b_router).then_inc(s_router, 16)
                if n == len(parts) - 1:
                    load_xT(Group(0, 1))
                if n >= 2:
                    sp.wait_ge(w_low, n - 1)
                sp.dma_start(stage[n % 2][:, 0:width], src).then_inc(s_stage[n % 2], 16)
            sp.wait_ge(w_low, len(parts))
            load_x(Group(0, 1))
            load_xT(Group(0, 2))

            with sp.Fori(1, BATCH) as b:
                load_x(Group(b, 0))
                store(Group(b, -2))
                load_xT(Group(b, 1))
                load_x(Group(b, 1))
                store(Group(b, -1))
                load_xT(Group(b, 2))
            store(Group(BATCH, -2))
            store(Group(BATCH, -1))
            sp.wait_ge(s_out, 16 * NG)

        @block.tensor
        def _(pe):
            def split_product(o, pairs):
                for k, (lhsT, rhs) in enumerate(pairs):
                    last = pe.matmul(o, lhsT, rhs, start=(k == 0), stop=(k == len(pairs) - 1))
                return last

            def project(g, t, j, bank, done):
                q = t % 2
                pairs = [(a[:, q, k, :], w[:, j, k, :]) for a, w in ((x_h, watt_h), (x_h, watt_l), (x_l, watt_h))
                         for k in range(KC)]
                split_product(A[:, bank, :], pairs).then_inc(done, 1)

            def group(ga, gf):
                for part, t, g in schedule(ga, gf):
                    c = TPG * g.p + t
                    if part == "QK":
                        pe.wait_ge(x_low, g.tiles(t))
                        if g.first() and t == 0:
                            pe.wait_ge(w_low, 1)
                        if positive(g.states(c)):
                            pe.wait_ge(state_upd, g.states(c))
                        project(g, t, 0, 0, qk_proj)
                    elif part == "V":
                        if g.first() and t == 0:
                            pe.wait_ge(w_low, 2)
                        project(g, t, 1, 1, v_proj)
                    elif part == "X1T":
                        pe.wait_ge(x1_sb, g.tiles(t))
                        for k in range(KC):
                            last = pe.transpose(A[:, 3, k * P:(k + 1) * P], x1[:, g.p, t, k * P:(k + 1) * P], ident)
                        last.then_inc(x1T_ps, 1)
                    elif part == "G":
                        if g.first() and t == 0:
                            pe.wait_ge(w_low, 3)
                        if positive(g.tiles(t - 1)):
                            pe.wait_ge(gated_sb, g.tiles(t - 1, HG))
                        project(g, t, 2, 2, g_proj)
                    elif part == "LOGITS":
                        pe.wait_ge(x1T_sb, g.tiles(t))
                        if g.first() and t == 0:
                            pe.wait_ge(s_router, 32)
                        if ga:
                            pe.wait_ge(qk_scaled, g.tiles(t + 1))
                        for k in range(KC):
                            last = pe.matmul(A[:, 0, 0:EXPERTS], x1T[:, k, :], wr[:, k, :],
                                             start=(k == 0), stop=(k == KC - 1))
                        last.then_inc(logits_ps, 1)
                    elif part == "QKT":
                        pe.wait_ge(qk_rot, g.tiles(t))
                        pe.wait_ge(gate_sb, g.tiles(t))
                        for k in range(4):
                            last = pe.transpose(A[:, 2, k * P:(k + 1) * P], qk[:, t % 2, k * P:(k + 1) * P], ident)
                        last.then_inc(qkT_ps, 1)
                    elif part == "SCORES":
                        pe.wait_ge(qkT_sb, g.tiles(t))
                        if positive(g.tiles(t - 1)):
                            pe.wait_ge(logits_sb, g.tiles(t - 1))
                            pe.wait_ge(x1T_low, g.tiles(t - 1))
                        pe.wait_ge(v_sb, g.tiles(t))
                        for h in range(HEADS):
                            r, m = h % 4, h // 4
                            last = pe.matmul(A[:, r, m * P:(m + 1) * P], qkT[r * KD:(r + 1) * KD, HG + m, :],
                                             qkT[r * KD:(r + 1) * KD, m, :], start=True, stop=True,
                                             tile_position=(r * KD, 0))
                        last.then_inc(scores_ps, 1)
                    elif part == "OUT":
                        pe.wait_ge(scores_sb, g.tiles(t, 2))
                        if c:
                            pe.wait_ge(state_sb, g.states(c, HG))
                        for m in range(HG):
                            if c:
                                pe.matmul(A[:, 2 + m, 0:OW], qkT[:, m, :], state[:, m, :], start=True, stop=False,
                                          skip_group_check=True)
                            for r in range(4):
                                last = pe.matmul(A[:, 2 + m, r * HE:(r + 1) * HE], scores[:, r, m, :],
                                                 v[:, 4 * m + r, :], start=(c == 0 and r == 0), stop=(r == 3),
                                                 skip_group_check=True)
                        last.then_inc(out_ps, 1)
                        if c < CHUNKS - 1:
                            for m in range(HG):
                                last = pe.matmul(A[:, m, 0:OW], qk[:, t % 2, (HG + m) * P:(HG + m + 1) * P],
                                                 v[:, 4 * m:4 * m + 4, :].rearrange("p h e -> p (h e)"),
                                                 start=True, stop=True)
                            last.then_inc(state_ps, 1)
                    elif part == "YT":
                        pe.wait_ge(y_sb, g.tiles(t))
                        for k in range(VC):
                            last = pe.transpose(A[:, 3, k * P:(k + 1) * P], y[:, k * P:(k + 1) * P], ident)
                        last.then_inc(yT_ps, 1)
                    elif part == "WO":
                        pe.wait_ge(yT_low, g.tiles(t))
                        if g.first() and t == 0:
                            pe.wait_ge(w_low, FIRST_PARTS)
                        o = A[:, 3, 0:D]
                        for w in (wo_h, wo_l):
                            for k in range(VC):
                                pe.matmul(o, yT_h[:, k, :], w[:, k, :], start=(w is wo_h and k == 0), stop=False)
                        for k in range(VC):
                            last = pe.matmul(o, yT_l[:, k, :], wo_h[:, k, :], start=False, stop=(k == VC - 1))
                        last.then_inc(wo_ps, 1)
                    elif part in ("H1", "H3"):
                        i, w = t, (w1 if part == "H1" else w3)
                        if part == "H1":
                            if i == 0:
                                pe.wait_ge(x1T_low, g.tiles(TPG - 1))
                                if g.first():
                                    pe.wait_ge(w_low, len(parts))
                            if positive(g.experts(i - 1)):
                                pe.wait_ge(act1_sb, g.experts(i - 1))
                        else:
                            if positive(g.experts(i - 1)):
                                pe.wait_ge(hid_sb, g.experts(i - 1))
                        pairs = [(w(wf, i, k), a[:, g.p, k, :]) for wf, a in ((wf_h, x1_h), (wf_l, x1_h), (wf_h, x1_l))
                                 for k in range(KC)]
                        split_product(F[:, 0 if part == "H1" else 1, :], pairs).then_inc(
                            h1_ps if part == "H1" else h3_ps, 1)
                    elif part == "W":
                        i = t
                        pe.wait_ge(hid_low, g.experts(i))
                        if positive(g.experts(i - (2 if i == 1 else 1), 4)):
                            pe.wait_ge(sum_sb, g.experts(i - (2 if i == 1 else 1), 4))
                        for s in range(TPG):
                            cut = slice(s * P, (s + 1) * P)
                            pairs = [(a[:, e % 2, cut], w2(w, e)) for e in ((0, 1) if i == 1 else (i,))
                                     for a, w in ((hid_h, wf_h), (hid_h, wf_l), (hid_l, wf_h))]
                            last = split_product(F[:, 2 + s // 2, (s % 2) * D:(s % 2 + 1) * D], pairs)
                            if s % 2:
                                last.then_inc(ffn_ps, 2 if i == 1 else 1)

            pe.wait_ge(s_cst, 16)
            whole_run(pe, group)

        @block.scalar
        def _(act):
            def split_x(g, t):
                if t == 0:
                    act.wait_ge(s_xT, g.groups(16))
                if positive(g.tiles(t - 2)):
                    act.wait_ge(g_proj, g.tiles(t - 2))
                act.activation(x_h[:, t % 2, :, :], xraw[:, :, t * P:(t + 1) * P], ACT.Copy).then_inc(x_high, 1)

            def next_x(g, t):
                if t < TPG - 1:
                    split_x(g, t + 1)
                else:
                    split_x(Group(g.b, g.at + 1), 0)

            def weight(n):
                _, width, high, _ = parts[n]
                act.wait_ge(s_stage[n % 2], 16 * (n // 2 + 1))
                act.activation(high, stage[n % 2][:, 0:width], ACT.Copy).then_inc(w_high, 1)

            def group(ga, gf):
                for part, t, g in schedule_of("scalar", ga, gf):
                    if part == "V":
                        act.wait_ge(v_proj, g.tiles(t))
                        act.activation(v[:, :, 0:HD], A[:, 1, :].rearrange("p (h e) -> p h e", h=HEADS),
                                       ACT.Copy).then_inc(v_sb, 1)
                    elif part == "X1T":
                        act.wait_ge(x1T_ps, g.tiles(t))
                        src = A[:, 3, 0:D].rearrange("p (k n) -> p k n", k=KC)
                        act.activation(x1T[:, :, :], src, ACT.Copy).then_inc(x1T_sb, 1)
                        if t == 0 and positive(g.before(2).experts(NE - 1)):
                            act.wait_ge(h3_ps, g.before(2).experts(NE - 1))
                        act.activation(x1_h[:, g.p, :, t * P:(t + 1) * P], src, ACT.Copy).then_inc(x1T_high, 1)
                    elif part == "G":
                        act.wait_ge(g_proj, g.tiles(t))
                        if positive(g.tiles(t - 1)):
                            act.wait_ge(gated_sb, g.tiles(t - 1, HG))
                        act.activation(gate[:, :], A[:, 2, :], ACT.Silu).then_inc(gate_sb, 1)
                    elif part == "LOGITS" and t == TPG - 1:
                        act.wait_ge(offset_sb, g.groups())
                        act.activation(share[:, :, :], offset[:, :, :], ACT.Tanh).then_inc(share_sb, 1)
                    elif part == "QKT":
                        act.wait_ge(qkT_ps, g.tiles(t))
                        if positive(g.tiles(t - 1)):
                            act.wait_ge(out_ps, g.tiles(t - 1))
                        act.activation(qkT[:, :, :], A[:, 2, :].rearrange("p (k n) -> p k n", k=4),
                                       ACT.Copy).then_inc(qkT_sb, 1)
                        next_x(g, t)
                    elif part == "OUT":
                        act.wait_ge(out_ps, g.tiles(t))
                        if positive(g.tiles(t - 1)):
                            act.wait_ge(meansq_sb, g.tiles(t - 1))
                        act.activation(squares[:, :, :].rearrange("p (m r) e -> p m (r e)", m=HG), A[:, 2:4, 0:OW],
                                       ACT.Square, scale=float(HD) ** -0.5).then_inc(sq_sb, 1)
                        if gf is None:
                            for n in range(FIRST_PARTS + 3 * t, min(FIRST_PARTS + 3 * t + 3, len(parts))):
                                weight(n)
                    elif part == "YT":
                        act.wait_ge(yT_ps, g.tiles(t))
                        act.activation(yT_h[:, :, :], A[:, 3, :].rearrange("p (k n) -> p k n", k=VC),
                                       ACT.Copy).then_inc(yT_high, 1)
                    elif part == "H1":
                        act.wait_ge(h1_ps, g.experts(t))
                        if positive(g.experts(t - 1)):
                            act.wait_ge(hid_sb, g.experts(t - 1))
                        act.activation(act1[:, :], F[:, 0, :], ACT.Silu).then_inc(act1_sb, 1)
                    elif part == "H3":
                        act.wait_ge(hid_sb, g.experts(t))
                        if positive(g.down(t - 2)):
                            act.wait_ge(ffn_ps, g.down(t - 2))
                        act.activation(hid_h[:, t % 2, :], hid[:, t % 2, :], ACT.Copy).then_inc(hid_high, 1)

            weight(0)
            split_x(Group(0, 0), 0)
            for n in range(1, FIRST_PARTS):
                weight(n)
            whole_run(act, group)

        @block.gpsimd
        def _(pool):
            def split_x(g, t):
                pool.wait_ge(x_high, g.tiles(t))
                if positive(g.tiles(t - 2)):
                    pool.wait_ge(g_proj, g.tiles(t - 2))
                pool.tensor_tensor(x_l[:, t % 2, :, :], xraw[:, :, t * P:(t + 1) * P],
                                   x_h[:, t % 2, :, :].bitcast(f32), ALU.subtract).then_inc(x_low, 1)

            def next_x(g, t):
                if t < TPG - 1:
                    split_x(g, t + 1)
                else:
                    split_x(Group(g.b, g.at + 1), 0)

            def group(ga, gf):
                for part, t, g in schedule_of("gpsimd", ga, gf):
                    c = TPG * g.p + t
                    if part == "QK":
                        pool.wait_ge(qk_scaled, g.tiles(t))
                        if positive(g.tiles(t - 1)):
                            pool.wait_ge(qk_rot, g.tiles(t - 1))
                        src = qk_s[:, :].rearrange("p (h k) -> p h k", k=KD)
                        dst = qk_w[:, :].rearrange("p (h k) -> p h k", k=KD)
                        half = KD // 2
                        for lo, hi in ((0, half), (half, KD)):
                            s = sin[:, c:c + 1, lo:hi].to_broadcast([P, 2 * HEADS, half])
                            pool.tensor_tensor(dst[:, :, lo:hi], src[:, :, half - lo:KD - lo], s,
                                               ALU.mult).then_inc(qk_sin, 1)
                    elif part == "QKT":
                        next_x(g, t)
                    elif part == "OUT":
                        pool.wait_ge(meansq_sb, g.tiles(t))
                        if positive(g.tiles(t - 1)):
                            pool.wait_ge(y_sb, g.tiles(t - 1))
                        pool.tensor_tensor(rms[:, :], meansq[:, :], minus_half[:, :], ALU.pow).then_inc(rms_sb, 1)
                    elif part == "WO":
                        pool.wait_ge(var_sb, g.tiles(t))
                        if positive(g.tiles(t - 1)):
                            pool.wait_ge(x1_sb, g.tiles(t - 1))
                        pool.tensor_tensor(rstd[:, :], var_eps[:, :], minus_half[:, 0:1], ALU.pow).then_inc(rstd_sb, 1)
                    elif part == "H3":
                        pool.wait_ge(hid_high, g.experts(t))
                        if positive(g.down(t - 2)):
                            pool.wait_ge(ffn_ps, g.down(t - 2))
                        pool.tensor_tensor(hid_l[:, t % 2, :], hid[:, t % 2, :], hid_h[:, t % 2, :].bitcast(f32),
                                           ALU.subtract).then_inc(hid_low, 1)
                    elif part == "W" and t == NE - 1:
                        pool.wait_ge(var2_sb, g.groups())
                        pool.tensor_tensor(rstd2[:, :], var_eps2[:, :], minus_half[:, 0:TPG], ALU.pow)\
                            .then_inc(rstd2_sb, 1)

            pool.memset(minus_half[:, :], -0.5).then_inc(ready0, 1)
            pool.memset(v[:, :, HD:HE], 1.0).then_inc(ready0, 1)
            pool.memset(logits[:, :, EXPERTS:], PAD).then_inc(ready0, 1)
            pool.memset(top2[:, :, 2:8], PAD).then_inc(ready0, 1)
            pool.wait_ge(ready0, 4)
            pool.wait_ge(s_cst, 16)
            split_x(Group(0, 0), 0)
            whole_run(pool, group)

        @block.vector
        def _(dve):
            def weight(n):
                _, width, high, low = parts[n]
                dve.wait_ge(w_high, n + 1)
                dve.tensor_tensor(low, stage[n % 2][:, 0:width], high.bitcast(f32), ALU.subtract).then_inc(w_low, 1)

            def group(ga, gf):
                for part, t, g in schedule_of("vector", ga, gf):
                    c = TPG * g.p + t
                    if part == "QK":
                        dve.wait_ge(qk_proj, g.tiles(t))
                        if positive(g.tiles(t - 1)):
                            dve.wait_ge(qk_sin, g.tiles(t - 1, 2))
                        heads = lambda a: a.rearrange("p (h k) -> p h k", k=KD)
                        dve.tensor_tensor(heads(qk_s[:, :]), heads(A[:, 0, :]),
                                          gamma.unsqueeze(2).to_broadcast([P, 2 * HEADS, KD]),
                                          ALU.mult).then_inc(qk_scaled, 1)
                        dve.wait_ge(qk_scaled, g.tiles(t))
                        dve.tensor_tensor(heads(qk_c[:, :]), heads(qk_s[:, :]),
                                          cos[:, c:c + 1, :].to_broadcast([P, 2 * HEADS, KD]),
                                          ALU.mult).then_inc(qk_cos, 1)
                    elif part == "G":
                        dve.wait_ge(qk_cos, g.tiles(t))
                        dve.wait_ge(qk_sin, g.tiles(t, 2))
                        dve.tensor_tensor(qk[:, t % 2, :], qk_c[:, :], qk_w[:, :], ALU.add).then_inc(qk_rot, 1)
                    elif part == "X1T":
                        dve.wait_ge(x1T_high, g.tiles(t))
                        cut = slice(t * P, (t + 1) * P)
                        dve.tensor_tensor(x1_l[:, g.p, :, cut], A[:, 3, 0:D].rearrange("p (k n) -> p k n", k=KC),
                                          x1_h[:, g.p, :, cut].bitcast(f32), ALU.subtract).then_inc(x1T_low, 1)
                    elif part == "LOGITS":
                        dve.wait_ge(logits_ps, g.tiles(t))
                        dve.tensor_tensor(logits[:, t, 0:EXPERTS], A[:, 0, 0:EXPERTS], br[:, :],
                                          ALU.add).then_inc(logits_sb, 1)
                        if t == TPG - 1:
                            route(g)
                    elif part == "SCORES":
                        dve.wait_ge(scores_ps, g.tiles(t))
                        for m in range(2):
                            dve.tensor_tensor(
                                scores[:, 2 * m:2 * m + 2, :, :].rearrange("p b m n -> p (b m) n"),
                                A[:, 2 * m:2 * m + 2, 0:2 * P].rearrange("p b (m n) -> p b m n", m=2),
                                causal.unsqueeze(1).to_broadcast([P, 4, P]), ALU.mult).then_inc(scores_sb, 1)
                    elif part == "OUT":
                        retention_out(g, t, c)
                        if gf is None:
                            for n in range(FIRST_PARTS + 3 * t, min(FIRST_PARTS + 3 * t + 3, len(parts))):
                                weight(n)
                    elif part == "NORM":
                        retention_norm(g, t)
                    elif part == "YT":
                        dve.wait_ge(yT_high, g.tiles(t))
                        dve.tensor_tensor(yT_l[:, :, :], A[:, 3, :].rearrange("p (k n) -> p k n", k=VC),
                                          yT_h[:, :, :].bitcast(f32), ALU.subtract).then_inc(yT_low, 1)
                    elif part == "WO":
                        layer_norm(g, t)
                    elif part == "X1":
                        layer_norm_apply(g, t)
                    elif part == "H3":
                        dve.wait_ge(act1_sb, g.experts(t))
                        dve.wait_ge(h3_ps, g.experts(t))
                        if positive(g.experts(max(t - 2, -1))):
                            dve.wait_ge(hid_low, g.experts(max(t - 2, -1)))
                        dve.tensor_tensor(hid[:, t % 2, :], F[:, 1, :], act1[:, :], ALU.mult).then_inc(hid_sb, 1)
                    elif part in ("SUM1", "SUM2"):
                        add_expert(g, t, 0 if part == "SUM1" else 1)
                        if (part, t) == ("SUM2", NE - 1):
                            moments_out(g)
                    elif part == "RESULT":
                        layer_norm_out(g)

            def hold():
                dve.sem_inc(held, 1)

            def retention_out(g, t, c):
                four = lambda a: a.rearrange("p (r e) -> p r e", e=HE)
                if c < CHUNKS - 1:
                    dve.wait_ge(state_ps, g.states(c + 1))
                    if positive(g.states(c, HG)):
                        dve.wait_ge(state_sb, g.states(c, HG))
                    dve.tensor_tensor(state_new[:, :, :], A[:, 0:2, 0:OW], block_decay, ALU.mult)\
                        .then_inc(state_upd, 1)
                dve.wait_ge(sq_sb, g.tiles(t))
                dve.tensor_reduce(sumsq[:, :], squares[:, :, 0:HD], AX.X, ALU.add).then_inc(norm_step, 1)
                dve.tensor_tensor(denom[:, :], squares[:, :, HD], rowsum[:, c, :], ALU.max).then_inc(norm_step, 1)
                dve.wait_ge(norm_step, g.tiles(t, 2))
                dve.scalar_tensor_tensor(meansq[:, :], denom[:, :], HD * EPS, sumsq[:, :], ALU.mult,
                                         ALU.add).then_inc(meansq_sb, 1)
                dve.wait_ge(gate_sb, g.tiles(t))
                for m in range(HG):
                    dve.tensor_tensor(gated[:, m * 4 * HD:(m + 1) * 4 * HD].rearrange("p (r e) -> p r e", e=HD),
                                      four(A[:, 2 + m, 0:OW])[:, :, 0:HD],
                                      gate[:, m * 4 * HD:(m + 1) * 4 * HD].rearrange("p (r e) -> p r e", e=HD),
                                      ALU.mult).then_inc(gated_sb, 1)
                if c < CHUNKS - 1:
                    dve.wait_ge(state_upd, g.states(c + 1))
                    if c == 0:
                        dve.tensor_copy(state[:, :, :], state_new[:, :, :]).then_inc(state_sb, HG)
                    else:
                        for m in range(HG):
                            dve.scalar_tensor_tensor(state[:, m, :], state[:, m, :], gamma_chunk[:, m:m + 1],
                                                     state_new[:, m, :], ALU.mult, ALU.add).then_inc(state_sb, 1)

            def retention_norm(g, t):
                dve.wait_ge(rms_sb, g.tiles(t))
                dve.wait_ge(gated_sb, g.tiles(t, HG))
                dve.tensor_tensor(y[:, :].rearrange("p (h e) -> p h e", e=HD),
                                  gated[:, :].rearrange("p (h e) -> p h e", e=HD),
                                  rms[:, :].unsqueeze(2).to_broadcast([P, HEADS, HD]), ALU.mult).then_inc(y_sb, 1)

            def layer_norm(g, t):
                dve.wait_ge(wo_ps, g.tiles(t))
                if t == 0:
                    dve.wait_ge(s_x[g.p], g.rows(16))
                dve.tensor_tensor(res[:, :], A[:, 3, 0:D], xres[:, g.p, t, :], ALU.add).then_inc(ln_step, 1)
                dve.wait_ge(ln_step, g.tiles(t, 3) - 2)
                dve.bn_stats(stats[:, :], res[:, :]).then_inc(ln_step, 1)
                dve.wait_ge(ln_step, g.tiles(t, 3) - 1)
                hold()
                dve.bn_aggr(moments[:, :], stats[:, :]).then_inc(ln_step, 1)
                dve.wait_ge(ln_step, g.tiles(t, 3))
                dve.tensor_scalar(var_eps[:, :], moments[:, 1:2], EPS, None, ALU.add).then_inc(var_sb, 1)

            def layer_norm_apply(g, t):
                dve.wait_ge(rstd_sb, g.tiles(t))
                if t == 0 and positive(g.groups(16, -1)):
                    dve.wait_ge(s_out, g.groups(16, -1))
                dve.tensor_scalar(x1[:, g.p, t, :], res[:, :], moments[:, 0:1], rstd[:, :], ALU.subtract,
                                  ALU.mult).then_inc(x1_sb, 1)

            def route(g):
                n = lambda k: g.groups(2 * TPG + 6, 0) + k
                dve.wait_ge(logits_sb, g.tiles(TPG - 1))
                hold()
                for s in range(TPG):
                    dve.max(top8[:, s, :], logits[:, s, 0:EXPERTS]).then_inc(route_step, 1)
                dve.wait_ge(route_step, n(TPG))
                dve.tensor_copy(top2[:, :, 0:2], top8[:, :, 0:2]).then_inc(route_step, 1)
                dve.tensor_tensor(middle[:, :], top8[:, :, 0], top8[:, :, 1], ALU.add).then_inc(route_step, 1)
                dve.wait_ge(route_step, n(TPG + 2))
                dve.scalar_tensor_tensor(offset[:, :, :], middle[:, :].unsqueeze(2).to_broadcast([P, TPG, EXPERTS]),
                                         -0.5, logits[:, :, 0:EXPERTS], ALU.mult, ALU.add).then_inc(offset_sb, 1)
                for s in range(TPG):
                    dve.match_replace(without[:, s, :], top2[:, s, :], logits[:, s, :], -PAD).then_inc(route_step, 1)
                dve.wait_ge(route_step, n(2 * TPG + 2))
                dve.tensor_tensor(chosen[:, :, :], logits[:, :, 0:EXPERTS], without[:, :, 0:EXPERTS],
                                  ALU.not_equal).then_inc(route_step, 1)
                dve.wait_ge(share_sb, g.groups())
                dve.tensor_scalar(half_share[:, :, :], share[:, :, :], 0.5, 0.5, ALU.mult, ALU.add)\
                    .then_inc(route_step, 1)
                dve.wait_ge(route_step, n(2 * TPG + 4))
                dve.tensor_tensor(gates[:, g.p, :, :], half_share[:, :, :], chosen[:, :, :], ALU.mult)\
                    .then_inc(route_step, 2)

            def add_expert(g, i, half):
                dve.wait_ge(ffn_ps, g.down(i) - 1 + half if i > 1 else g.down(i) - 2 + 2 * half)
                if i == 1:
                    acc = x1[:, g.p, 2 * half:2 * half + 2, :].rearrange("p t d -> p (t d)")
                    dve.tensor_tensor(acc, F[:, 2 + half, :], acc, ALU.add).then_inc(sum_sb, 4)
                    return
                if i == 2 and not half:
                    dve.wait_ge(route_step, g.groups(2 * TPG + 6))
                for s in (2 * half, 2 * half + 1):
                    dve.wait_ge(sum_sb, g.experts(1, 4) - 4 + 4 * half if i == 2 else g.experts(i - 1, 4) + s + 1 - TPG)
                    dve.scalar_tensor_tensor(x1[:, g.p, s, :], F[:, 2 + half, (s % 2) * D:(s % 2 + 1) * D],
                                             gates[:, g.p, s, i - SHARED:i - SHARED + 1], x1[:, g.p, s, :],
                                             ALU.mult, ALU.add).then_inc(sum_sb, 1)

            def moments_out(g):
                for s in range(TPG):
                    dve.wait_ge(sum_sb, g.experts(NE - 1, 4) + s + 1 - TPG)
                    dve.bn_stats(stats2[:, s, :], x1[:, g.p, s, :]).then_inc(ln2_step, 1)
                for s in range(TPG):
                    dve.wait_ge(ln2_step, g.groups(2 * TPG, 0) + s + 1)
                    hold()
                    dve.bn_aggr(moments2[:, s, :], stats2[:, s, :]).then_inc(ln2_step, 1)
                dve.wait_ge(ln2_step, g.groups(2 * TPG))
                dve.tensor_scalar(var_eps2[:, :], moments2[:, :, 1], EPS, None, ALU.add).then_inc(var2_sb, 1)

            def layer_norm_out(g):
                dve.wait_ge(rstd2_sb, g.groups())
                for s in range(TPG):
                    dve.tensor_scalar(x1[:, g.p, s, :], x1[:, g.p, s, :], moments2[:, s, 0:1], rstd2[:, s:s + 1],
                                      ALU.subtract, ALU.mult).then_inc(result_sb, 1)

            for n in range(FIRST_PARTS):
                weight(n)
            dve.wait_ge(ready0, 4)
            dve.wait_ge(s_cst, 16)
            dve.wait_ge(s_router, 32)
            whole_run(dve, group)


def shape_constants():
    f = np.float32
    lin = np.linspace(0.0, 1.0, KD // 2).astype(f)
    angle = (f(1.0) / np.power(f(10000.0), lin)).astype(f)
    pos = np.arange(SEQ, dtype=f)
    arg = (pos[:, None] * angle[None, :]).astype(f).astype(np.float64)
    s, c = np.sin(arg), np.cos(arg)
    decay = np.log1p(-2.0 ** (-5.0 - np.arange(HEADS, dtype=np.float64)))
    i = np.arange(P, dtype=np.float64)
    t = {}
    grow = np.exp(i[:, None] * decay[None, :])
    t["gamma"] = np.concatenate([grow, float(KD) ** -0.5 / grow], 1)
    by_chunk = lambda a: a.reshape(CHUNKS, P, -1).transpose(1, 0, 2).reshape(P, -1)
    t["cos"] = by_chunk(np.concatenate([c, c], 1))
    t["sin"] = by_chunk(np.concatenate([-s, s], 1))
    t["causal"] = (i[:, None] <= i[None, :]).astype(np.float64)
    block = np.zeros((P, HG, OW))
    per_chunk = np.exp(P * decay)
    for h in range(HEADS):
        m, r = h // 4, h % 4
        block[r * KD:(r + 1) * KD, m, r * HE:(r + 1) * HE] = per_chunk[h]
    t["block"] = block.reshape(P, -1)
    t["gamma_chunk"] = np.repeat(per_chunk.reshape(HG, 4).T, KD, axis=0)
    rows = np.cumsum(np.exp(np.arange(SEQ)[:, None] * decay[None, :]), 0)
    t["rowsum"] = by_chunk(rows / HD)
    t["ident"] = np.eye(P)
    return np.concatenate([t[name].reshape(P, width) for name, width in CONST_WIDTHS], 1).astype(f)


def kernel(**inputs):
    import numpy as _np
    import concourse.bacc as _bacc
    from concourse import mybir as _mybir
    from concourse.bass_utils import run_bass_kernel_spmd as _run

    a = {k.removeprefix("L0_"): _np.asarray(v) for k, v in inputs.items()}
    x = a["attn_x"].reshape(BATCH * SEQ, D)
    even_odd = _np.arange(D).reshape(HEADS, KD // 2, 2).transpose(0, 2, 1).reshape(-1)
    rows = lambda w: w.reshape(-1, P, w.shape[-1]).transpose(1, 0, 2)
    flat = lambda w: rows(w).reshape(P, -1)
    qk = _np.concatenate([a["attn_wq"][:, even_odd], a["attn_wk"][:, even_odd]], 1)
    experts = [(a["ffn_shared_w1"][e], a["ffn_shared_w3"][e], a["ffn_shared_w2"][e]) for e in range(SHARED)]
    experts += [(a["ffn_routed_w1"][e], a["ffn_routed_w3"][e], a["ffn_routed_w2"][e]) for e in range(EXPERTS)]
    arrays = {
        "x": x,
        "xT": _np.concatenate([x, x[:GT]]).reshape(NG + 1, GT, KC, P).transpose(0, 3, 2, 1),
        "w_att": _np.stack([flat(w) for w in (qk, a["attn_wv"], a["attn_wg"])]),
        "w_wo": flat(a["attn_wo"]),
        "w_ffn": _np.stack([_np.concatenate([flat(m) for m in e], 1) for e in experts]),
        "w_router": rows(a["ffn_router_w"]),
        "b_router": _np.repeat(a["ffn_router_b"][None, :], P, 0),
        "consts": shape_constants(),
    }
    arrays = {k: _np.ascontiguousarray(v) for k, v in arrays.items()}

    nc = _bacc.Bacc("TRN2", target_bir_lowering=False, num_devices=1)
    args = [nc.dram_tensor(k, v.shape, _mybir.dt.from_np(v.dtype), kind="ExternalInput").ap()
            for k, v in arrays.items()]
    out = nc.dram_tensor("out", (BATCH * SEQ, D), _mybir.dt.float32, kind="ExternalOutput").ap()
    retention_moe_kernel(nc, *args, out)
    r = _run(nc, [arrays], core_ids=[0])
    return r.results[0]["out"].reshape(BATCH, SEQ, D)
```

```python
import math
from contextlib import ExitStack

import numpy as np

import concourse.bass as bass
from concourse import mybir

BATCH, SEQ, D = 8, 1024, 256
HEADS, KD, HD = 8, 32, 64
VD = HEADS * HD
EXPERTS, SHARED, HID = 8, 2, 128
EPS = 1e-5

P = 128
TPG = 4
GPB = SEQ // (P * TPG)
CHUNKS = SEQ // P
NG = BATCH * GPB
GT = TPG * P
KC = D // P
VC = VD // P
HG = HEADS // 4
HE = HD + 1
OW = 4 * HE
NE = SHARED + EXPERTS
EW = KC * HID * 2 + D
PROJ = 3
FIRST_PARTS = PROJ + 1
PAD = 3.0e38

CONST_WIDTHS = [("gamma", 2 * HEADS), ("cos", CHUNKS * KD), ("sin", CHUNKS * KD), ("causal", P),
                ("block", HG * OW), ("gamma_chunk", HG), ("rowsum", CHUNKS * HEADS), ("ident", P)]
CONST_AT, _at = {}, 0
for _name, _width in CONST_WIDTHS:
    CONST_AT[_name] = (_at, _at + _width)
    _at += _width
CONSTS = _at

LATE = ("NORM", "YT", "WO", "X1", "X1T", "LOGITS")
SLOTS = [s.split() for s in (
    "NORM QK V YT G ROT WO F QKT X1 F X1T F LOGITS F SCORES F OUT F F",
    "NORM QK F V YT G ROT WO F QKT X1 X1T F LOGITS F SCORES F OUT F F",
    "NORM QK V YT G ROT WO F QKT X1 F X1T F LOGITS F SCORES F OUT F F F",
    "NORM QK V YT G ROT WO QKT X1 F F X1T F LOGITS F SCORES F OUT F F",
)]
PLACES = {
    "scalar": {"X1T": 0.5, "QKT": 1},
    "vector": {"SUM1": 0, "SUM2": 0, "NORM": -0.5, "X1": -1.5},
    "gpsimd": {},
}


FIRST_START = {
    "tensor": "QK V G",
    "scalar": "WEIGHT XS WEIGHT XS+ WEIGHT VS GS WEIGHT",
    "vector": "WEIGHT WEIGHT QK WEIGHT ROT WEIGHT",
    "gpsimd": "XS XS+ QK",
}
FIRST_SLOT = {
    "tensor": "QK+ LOGITS-- QKT V+ YT- SCORES WO- OUT X1T- G+",
    "scalar": "QKT XS++ YT- WEIGHT WEIGHT OUT VS+ X1T- WEIGHT GS+",
    "vector": "NORM- LOGITS-- QK+ YT- WEIGHT SCORES ROT+ WO- WEIGHT X1- X1T- OUT WEIGHT",
    "gpsimd": "QK+ XS++ WO- OUT",
}
FIRST_END = {"tensor": "LOGITS--", "scalar": "", "vector": "LOGITS--", "gpsimd": ""}


def last_steps(g):
    return [("H1", NE - 1, g), ("W", NE - 3, g), ("H3", NE - 1, g), ("W", NE - 2, g), ("W", NE - 1, g)]


def feed_forward_steps(g):
    steps = [(part, i, g) for part, i in (("H1", 0), ("H3", 0), ("H1", 1), ("H3", 1), ("H1", 2), ("W", 1), ("H3", 2))]
    for i in range(3, NE - 1):
        steps += [("H1", i, g), ("H3", i, g)] + ([("W", i - 1, g)] if i < NE - 2 else [])
    return steps


def schedule(ga, gf):
    out = []
    if not ga:
        for n, step in enumerate(last_steps(gf.before(1))):
            out += [step] + ([(LATE[n], TPG - 1, gf)] if n < 3 else [])
        out += [(part, TPG - 1, gf) for part in LATE[3:]] + [("RESULT", 0, gf.before(1))]
        return out + feed_forward_steps(gf) + last_steps(gf) + [("RESULT", 0, gf)]
    steps = [step if gf.before(1).exists() else None for step in last_steps(gf.before(1))]
    steps += feed_forward_steps(gf)
    for t in range(TPG):
        for part in SLOTS[t]:
            if part == "F":
                step = steps.pop(0) if steps else None
                if step:
                    out.append(step)
            elif part in LATE:
                out.append((part, t - 1, ga) if t else (part, TPG - 1, gf))
            else:
                out.append((part, t, ga))
                if part == "OUT" and t == 0 and gf.before(1).exists():
                    out.append(("RESULT", 0, gf.before(1)))
    return out + steps


def first_schedule(engine, ga):
    out, weights = [], list(range(FIRST_PARTS + NE))
    slots = [FIRST_START[engine]] + TPG * [FIRST_SLOT[engine]] + [FIRST_END[engine]]
    for t, slot in enumerate(slots, start=-1):
        for token in slot.split():
            part, at = token.strip("+-"), max(t, 0) + token.count("+") - token.count("-")
            if part == "WEIGHT":
                out += [(part, weights.pop(0), ga)] if weights else []
            elif part == "XS" and at == TPG:
                out.append((part, 0, Group(ga.b, ga.at + 1)))
            elif 0 <= at < TPG:
                out.append((part, at, ga))
    return out


def schedule_of(engine, ga, gf):
    if not gf:
        return first_schedule(engine, ga)
    parts, places = [], PLACES.get(engine, {})
    for n, (part, t, g) in enumerate(schedule(ga, gf)):
        halves = ("SUM1", "SUM2") if (engine, part) == ("vector", "W") else (part,)
        parts += [(n + places.get(p, 0), len(parts), (p, t, g)) for p in halves]
    return [p for _, _, p in sorted(parts, key=lambda x: x[:2])]


class Group:

    def __init__(self, b, at):
        self.b, self.at = b, at
        self.p = at % GPB

    def tiles(self, t, per=1):
        return self.b * (per * CHUNKS) + per * (TPG * self.at + t + 1)

    def experts(self, i, per=1):
        return self.b * (per * NE * GPB) + per * (NE * self.at + i + 1)

    def down(self, i):
        return self.experts(max(i, -1) or 1, 2)

    def groups(self, per=1, k=1):
        return self.b * (per * GPB) + per * (self.at + k)

    def rows(self, per):
        return self.b * per + per * (self.at // GPB + 1)

    def states(self, chunk, per=1, updates=CHUNKS - 1):
        return self.b * (per * updates) + per * (self.at // GPB * updates + chunk)

    def index(self):
        return self.b * GPB + self.at

    def first(self):
        return isinstance(self.b, int) and self.index() == 0

    def exists(self):
        return not isinstance(self.b, int) or self.index() >= 0

    def before(self, k):
        return Group(self.b, self.at - k)


def positive(value):
    return not isinstance(value, int) or value > 0


def retention_moe_kernel(nc, x, xT, w_att, w_wo, w_ffn, w_router, b_router, consts, out):
    f32, f32r = mybir.dt.float32, mybir.dt.float32r
    ALU, ACT, AX = mybir.AluOpType, mybir.ActivationFunctionType, mybir.AxisListType

    x_v = x.rearrange("(g t p) d -> g p t d", t=TPG, p=P)
    out_v = out.rearrange("(g t p) d -> g p t d", t=TPG, p=P)

    with ExitStack() as ctx:
        def sb(name, shape, dt=f32):
            return ctx.enter_context(nc.sbuf_tensor(name, shape, dt))

        def sem(name):
            return ctx.enter_context(nc.semaphore(name))

        watt_h, watt_l = sb("watt_h", [P, PROJ, KC, 512], f32r), sb("watt_l", [P, PROJ, KC, 512], f32r)
        wo_h, wo_l = sb("wo_h", [P, VC, D], f32r), sb("wo_l", [P, VC, D], f32r)
        wf_h, wf_l = sb("wf_h", [P, NE, EW], f32r), sb("wf_l", [P, NE, EW], f32r)
        wr = sb("wr", [P, KC, EXPERTS])
        br = sb("br", [P, EXPERTS])
        cst = sb("cst", [P, CONSTS])

        def const(name):
            return cst[:, CONST_AT[name][0]:CONST_AT[name][1]]

        gamma = const("gamma")
        cos = const("cos").rearrange("p (c k) -> p c k", c=CHUNKS)
        sin = const("sin").rearrange("p (c k) -> p c k", c=CHUNKS)
        causal = const("causal")
        block_decay = const("block").rearrange("p (g w) -> p g w", g=HG)
        gamma_chunk = const("gamma_chunk")
        rowsum = const("rowsum").rearrange("p (c h) -> p c h", c=CHUNKS)
        ident = const("ident")

        xraw = sb("xraw", [P, 2, KC, GT])
        x_h, x_l = sb("x_h", [P, 2, KC, P], f32r), sb("x_l", [P, 2, KC, P], f32r)
        xres = sb("xres", [P, 2, TPG, D])
        qk_s, qk_c, qk_w = sb("qk_s", [P, 512]), sb("qk_c", [P, 512]), sb("qk_w", [P, 512])
        qk = sb("qk", [P, 2, 512])
        qkT = sb("qkT", [P, 4, P])
        v = sb("v", [P, HEADS, HE])
        gate = sb("gate", [P, VD])
        scores = sb("scores", [P, 4, 2, P])
        state = sb("state", [P, HG, OW])
        state_new = sb("state_new", [P, HG, OW])
        squares = sb("squares", [P, HEADS, HE])
        sumsq, denom = sb("sumsq", [P, HEADS]), sb("denom", [P, HEADS])
        meansq, rms = sb("meansq", [P, HEADS]), sb("rms", [P, HEADS])
        minus_half = sb("minus_half", [P, HEADS])
        gated, y = sb("gated", [P, VD]), sb("y", [P, VD])
        yT_h, yT_l = sb("yT_h", [P, VC, P], f32r), sb("yT_l", [P, VC, P], f32r)
        res = sb("res", [P, D])
        stats, moments = sb("stats", [P, 6]), sb("moments", [P, 2])
        var_eps, rstd = sb("var_eps", [P, 1]), sb("rstd", [P, 1])
        x1 = sb("x1", [P, 2, TPG, D])
        x1T = sb("x1T", [P, KC, P])
        x1_h, x1_l = sb("x1_h", [P, 2, KC, GT], f32r), sb("x1_l", [P, 2, KC, GT], f32r)
        logits = sb("logits", [P, TPG, EXPERTS + 6])
        top8, top2 = sb("top8", [P, TPG, 8]), sb("top2", [P, TPG, 8])
        without = sb("without", [P, TPG, EXPERTS + 6])
        middle, offset = sb("middle", [P, TPG]), sb("offset", [P, TPG, EXPERTS])
        chosen, share = sb("chosen", [P, TPG, EXPERTS]), sb("share", [P, TPG, EXPERTS])
        half_share = sb("half_share", [P, TPG, EXPERTS])
        gates = sb("gates", [P, 2, TPG, EXPERTS])
        act1 = sb("act1", [P, GT])
        hid = sb("hid", [P, 2, GT])
        hid_h, hid_l = sb("hid_h", [P, 2, GT], f32r), sb("hid_l", [P, 2, GT], f32r)
        stats2, moments2 = sb("stats2", [P, TPG, 6]), sb("moments2", [P, TPG, 2])
        var_eps2, rstd2 = sb("var_eps2", [P, TPG]), sb("rstd2", [P, TPG])

        A = ctx.enter_context(nc.psum_tensor("A", [P, 4, 512], f32))
        F = ctx.enter_context(nc.psum_tensor("F", [P, 4, 512], f32))

        s_cst, s_router, s_out = sem("s_cst"), sem("s_router"), sem("s_out")
        s_stage = [sem("s_stage0"), sem("s_stage1"), sem("s_stage2")]
        s_xT, s_x = [sem("s_xT0"), sem("s_xT1")], [sem("s_x0"), sem("s_x1")]
        w_high, w_low = sem("w_high"), sem("w_low")
        ready0 = sem("ready0")
        x_high, x_low = sem("x_high"), sem("x_low")
        qk_proj, v_proj, g_proj = sem("qk_proj"), sem("v_proj"), sem("g_proj")
        qk_scaled, qk_cos, qk_sin, qk_rot = sem("qk_scaled"), sem("qk_cos"), sem("qk_sin"), sem("qk_rot")
        v_sb, gate_sb = sem("v_sb"), sem("gate_sb")
        qkT_ps, qkT_sb = sem("qkT_ps"), sem("qkT_sb")
        scores_ps, scores_sb = sem("scores_ps"), sem("scores_sb")
        out_ps, state_ps, state_upd, state_sb = sem("out_ps"), sem("state_ps"), sem("state_upd"), sem("state_sb")
        sq_sb, norm_step, meansq_sb, rms_sb = sem("sq_sb"), sem("norm_step"), sem("meansq_sb"), sem("rms_sb")
        gated_sb, y_sb = sem("gated_sb"), sem("y_sb")
        yT_ps, yT_high, yT_low = sem("yT_ps"), sem("yT_high"), sem("yT_low")
        wo_ps, ln_step, var_sb, rstd_sb, x1_sb = sem("wo_ps"), sem("ln_step"), sem("var_sb"), sem("rstd_sb"), sem("x1_sb")
        held = sem("held")
        x1T_ps, x1T_sb, x1T_high, x1T_low = sem("x1T_ps"), sem("x1T_sb"), sem("x1T_high"), sem("x1T_low")
        logits_ps, logits_sb = sem("logits_ps"), sem("logits_sb")
        route_step, offset_sb, share_sb = sem("route_step"), sem("offset_sb"), sem("share_sb")
        h1_ps, h3_ps, act1_sb, hid_sb, hid_high, hid_low = (sem("h1_ps"), sem("h3_ps"), sem("act1_sb"), sem("hid_sb"),
                                                            sem("hid_high"), sem("hid_low"))
        ffn_ps, sum_sb = sem("ffn_ps"), sem("sum_sb")
        ln2_step, var2_sb, rstd2_sb, result_sb = sem("ln2_step"), sem("var2_sb"), sem("rstd2_sb"), sem("result_sb")

        stage = [x1[:, 1, :, :].rearrange("p t d -> p (t d)"), xres[:, 1, :, :].rearrange("p t d -> p (t d)"),
                 hid[:, :, :].rearrange("p a n -> p (a n)")]
        parts = []
        for j in range(PROJ):
            parts.append((w_att[j], KC * 512, watt_h[:, j, :, :].rearrange("p k n -> p (k n)"),
                          watt_l[:, j, :, :].rearrange("p k n -> p (k n)")))
        parts.append((w_wo, VC * D, wo_h[:, :, :].rearrange("p k n -> p (k n)"),
                      wo_l[:, :, :].rearrange("p k n -> p (k n)")))
        for i in range(NE):
            parts.append((w_ffn[i], EW, wf_h[:, i, :], wf_l[:, i, :]))

        def w1(w, i, k):
            return w[:, i, k * HID:(k + 1) * HID]

        def w3(w, i, k):
            return w[:, i, (KC + k) * HID:(KC + k + 1) * HID]

        def w2(w, i):
            return w[:, i, 2 * KC * HID:EW]

        def banks(gf):
            if gf:
                return A[:, 0, :], A[:, 1, :], A[:, 2, :], A[:, 3, :], A[:, 1, 0:D], A[:, 0, 0:EXPERTS]
            return F[:, 2, :], F[:, 3, :], F[:, 1, :], F[:, 0, :], F[:, 0, 0:D], F[:, 0, D:D + EXPERTS]

        def whole_run(eng, group):
            group(Group(0, 0), None)
            group(Group(0, 1), Group(0, 0))
            with eng.Fori(1, BATCH) as b:
                group(Group(b, 0), Group(b, -1))
                group(Group(b, 1), Group(b, 0))
            group(None, Group(BATCH - 1, 1))

        block = ctx.enter_context(nc.Block())

        @block.sync
        def _(sp):
            def load_xT(g):
                if positive(g.groups(1, -1)):
                    sp.wait_ge(x_low, g.before(2).tiles(TPG - 1))
                sp.dma_start(xraw[:, g.p, :, :], xT[g.index()]).then_inc(s_xT[g.p], 16)

            def load_x(g):
                if positive(g.groups(1, -1)):
                    sp.wait_ge(ln_step, g.before(2).tiles(TPG - 1, 3))
                sp.dma_start(xres[:, g.p, :, :], x_v[g.index()]).then_inc(s_x[g.p], 16)

            def store(g):
                sp.wait_ge(result_sb, g.groups(TPG))
                sp.dma_start(out_v[g.index()], x1[:, g.p, :, :]).then_inc(s_out, 16)

            for n, (src, width, _, _) in enumerate(parts):
                if n == 1:
                    load_xT(Group(0, 0))
                if n == 2:
                    sp.dma_start(cst[:, :], consts).then_inc(s_cst, 16)
                if n == FIRST_PARTS:
                    load_x(Group(0, 0))
                    sp.dma_start(wr[:, :, :], w_router).then_inc(s_router, 16)
                    sp.dma_start(br[:, :], b_router).then_inc(s_router, 16)
                if n == FIRST_PARTS + 3:
                    load_xT(Group(0, 1))
                if n >= len(stage):
                    sp.wait_ge(w_low, n - len(stage) + 1)
                sp.dma_start(stage[n % len(stage)][:, 0:width], src).then_inc(s_stage[n % len(stage)], 16)
            sp.wait_ge(w_low, len(parts))
            load_x(Group(0, 1))
            load_xT(Group(0, 2))

            with sp.Fori(1, BATCH) as b:
                load_x(Group(b, 0))
                store(Group(b, -2))
                load_xT(Group(b, 1))
                load_x(Group(b, 1))
                store(Group(b, -1))
                load_xT(Group(b, 2))
            store(Group(BATCH, -2))
            store(Group(BATCH, -1))
            sp.wait_ge(s_out, 16 * NG)

        @block.tensor
        def _(pe):
            def split_product(o, pairs):
                for k, (lhsT, rhs) in enumerate(pairs):
                    last = pe.matmul(o, lhsT, rhs, start=(k == 0), stop=(k == len(pairs) - 1))
                return last

            def project(g, t, j, o, done):
                q = t % 2
                pairs = [(a[:, q, k, :], w[:, j, k, :]) for a, w in ((x_h, watt_h), (x_h, watt_l), (x_l, watt_h))
                         for k in range(KC)]
                split_product(o, pairs).then_inc(done, 1)

            def group(ga, gf):
                qk_bank, v_bank, g_bank, late_bank, wo_bank, logits_bank = banks(gf)
                for part, t, g in schedule_of("tensor", ga, gf):
                    c = TPG * g.p + t
                    if part == "QK":
                        pe.wait_ge(x_low, g.tiles(t))
                        if g.first() and t == 0:
                            pe.wait_ge(w_low, 1)
                        if gf:
                            if positive(g.states(c)):
                                pe.wait_ge(state_upd, g.states(c))
                        elif t:
                            pe.wait_ge(qk_scaled, g.tiles(t - 1))
                        project(g, t, 0, qk_bank, qk_proj)
                    elif part == "V":
                        if g.first() and t == 0:
                            pe.wait_ge(w_low, 2)
                        if not gf and t:
                            pe.wait_ge(v_sb, g.tiles(t - 1))
                        project(g, t, 1, v_bank, v_proj)
                    elif part == "X1T":
                        pe.wait_ge(x1_sb, g.tiles(t))
                        for k in range(KC):
                            last = pe.transpose(late_bank[:, k * P:(k + 1) * P], x1[:, g.p, t, k * P:(k + 1) * P], ident)
                        last.then_inc(x1T_ps, 1)
                    elif part == "G":
                        if g.first() and t == 0:
                            pe.wait_ge(w_low, 3)
                        if gf:
                            pe.wait_ge(gated_sb, g.tiles(t - 1, HG))
                        elif t:
                            pe.wait_ge(gate_sb, g.tiles(t - 1))
                        project(g, t, 2, g_bank, g_proj)
                    elif part == "LOGITS":
                        pe.wait_ge(x1T_sb, g.tiles(t))
                        if g.first() and t == 0:
                            pe.wait_ge(s_router, 32)
                        if ga and gf:
                            pe.wait_ge(qk_scaled, g.tiles(t + 1))
                        elif not gf:
                            pe.wait_ge(x1T_low, g.tiles(t))
                        for k in range(KC):
                            last = pe.matmul(logits_bank, x1T[:, k, :], wr[:, k, :],
                                             start=(k == 0), stop=(k == KC - 1))
                        last.then_inc(logits_ps, 1)
                    elif part == "QKT":
                        pe.wait_ge(qk_rot, g.tiles(t))
                        if g.first() and t == 0:
                            pe.wait_ge(s_cst, 16)
                        if gf:
                            pe.wait_ge(gate_sb, g.tiles(t))
                        elif t:
                            pe.wait_ge(gated_sb, g.tiles(t - 1, HG))
                        for k in range(4):
                            last = pe.transpose(A[:, 2, k * P:(k + 1) * P], qk[:, t % 2, k * P:(k + 1) * P], ident)
                        last.then_inc(qkT_ps, 1)
                    elif part == "SCORES":
                        pe.wait_ge(qkT_sb, g.tiles(t))
                        if gf:
                            pe.wait_ge(logits_sb, g.tiles(t - 1))
                            pe.wait_ge(x1T_low, g.tiles(t - 1))
                            pe.wait_ge(v_sb, g.tiles(t))
                        elif t:
                            pe.wait_ge(state_upd, g.states(c))
                        for h in range(HEADS):
                            r, m = h % 4, h // 4
                            last = pe.matmul(A[:, r, m * P:(m + 1) * P], qkT[r * KD:(r + 1) * KD, HG + m, :],
                                             qkT[r * KD:(r + 1) * KD, m, :], start=True, stop=True,
                                             tile_position=(r * KD, 0))
                        last.then_inc(scores_ps, 1)
                    elif part == "OUT":
                        pe.wait_ge(scores_sb, g.tiles(t, 2) - 1)
                        if c:
                            pe.wait_ge(state_sb, g.states(c, HG))
                            for m in range(HG):
                                pe.matmul(A[:, 2 + m, 0:OW], qkT[:, m, :], state[:, m, :], start=True, stop=False,
                                          skip_group_check=True)
                        if not gf:
                            pe.wait_ge(v_sb, g.tiles(t))
                        for r in (2, 3, 0, 1):
                            if r == 0:
                                pe.wait_ge(scores_sb, g.tiles(t, 2))
                            for m in range(HG):
                                last = pe.matmul(A[:, 2 + m, r * HE:(r + 1) * HE], scores[:, r, m, :],
                                                 v[:, 4 * m + r, :], start=(c == 0 and r == 2), stop=(r == 1),
                                                 skip_group_check=True)
                        last.then_inc(out_ps, 1)
                        if c < CHUNKS - 1:
                            for m in range(HG):
                                last = pe.matmul(A[:, m, 0:OW], qk[:, t % 2, (HG + m) * P:(HG + m + 1) * P],
                                                 v[:, 4 * m:4 * m + 4, :].rearrange("p h e -> p (h e)"),
                                                 start=True, stop=True)
                            last.then_inc(state_ps, 1)
                    elif part == "YT":
                        pe.wait_ge(y_sb, g.tiles(t))
                        if not gf and t:
                            pe.wait_ge(logits_sb, g.tiles(t - 1))
                        for k in range(VC):
                            last = pe.transpose(late_bank[:, k * P:(k + 1) * P], y[:, k * P:(k + 1) * P], ident)
                        last.then_inc(yT_ps, 1)
                    elif part == "WO":
                        if gf:
                            pe.wait_ge(yT_high, g.tiles(t))
                            if ga:
                                pe.wait_ge(v_sb, g.tiles(t + 1))
                        else:
                            pe.wait_ge(yT_low, g.tiles(t))
                        if g.first() and t == 0:
                            pe.wait_ge(w_low, FIRST_PARTS)
                        for w in (wo_h, wo_l):
                            for k in range(VC):
                                pe.matmul(wo_bank, yT_h[:, k, :], w[:, k, :], start=(w is wo_h and k == 0), stop=False)
                        pe.wait_ge(yT_low, g.tiles(t))
                        for k in range(VC):
                            last = pe.matmul(wo_bank, yT_l[:, k, :], wo_h[:, k, :], start=False, stop=(k == VC - 1))
                        last.then_inc(wo_ps, 1)
                    elif part in ("H1", "H3"):
                        i, w = t, (w1 if part == "H1" else w3)
                        if part == "H1":
                            if i == 0:
                                pe.wait_ge(x1T_low, g.tiles(TPG - 1))
                                if g.first():
                                    pe.wait_ge(w_low, len(parts))
                            if positive(g.experts(i - 1)):
                                pe.wait_ge(act1_sb, g.experts(i - 1))
                        else:
                            if positive(g.experts(i - 1)):
                                pe.wait_ge(hid_sb, g.experts(i - 1))
                        pairs = [(w(wf, i, k), a[:, g.p, k, :]) for wf, a in ((wf_h, x1_h), (wf_l, x1_h), (wf_h, x1_l))
                                 for k in range(KC)]
                        split_product(F[:, 0 if part == "H1" else 1, :], pairs).then_inc(
                            h1_ps if part == "H1" else h3_ps, 1)
                    elif part == "W":
                        i = t
                        pe.wait_ge(hid_low, g.experts(i))
                        before = i - (2 if i == 1 else 1)
                        for s in range(TPG):
                            if s % 2 == 0 and positive(g.experts(before, 4)):
                                pe.wait_ge(sum_sb, g.experts(before, 4) - ((4 if i == 2 else 2) if s == 0 else 0))
                            cut = slice(s * P, (s + 1) * P)
                            pairs = [(a[:, e % 2, cut], w2(w, e)) for e in ((0, 1) if i == 1 else (i,))
                                     for a, w in ((hid_h, wf_h), (hid_h, wf_l), (hid_l, wf_h))]
                            last = split_product(F[:, 2 + s // 2, (s % 2) * D:(s % 2 + 1) * D], pairs)
                            if s % 2:
                                last.then_inc(ffn_ps, 2 if i == 1 else 1)

            whole_run(pe, group)

        @block.scalar
        def _(act):
            def split_x(g, t):
                if t == 0:
                    act.wait_ge(s_xT[g.p], g.rows(16))
                if positive(g.tiles(t - 2)):
                    act.wait_ge(g_proj, g.tiles(t - 2))
                act.activation(x_h[:, t % 2, :, :], xraw[:, g.p, :, t * P:(t + 1) * P], ACT.Copy).then_inc(x_high, 1)

            def next_x(g, t):
                if t < TPG - 1:
                    split_x(g, t + 1)
                else:
                    split_x(Group(g.b, g.at + 1), 0)

            def weight(n):
                _, width, high, _ = parts[n]
                act.wait_ge(s_stage[n % len(stage)], 16 * (n // len(stage) + 1))
                act.activation(high, stage[n % len(stage)][:, 0:width], ACT.Copy).then_inc(w_high, 1)

            def group(ga, gf):
                _, v_bank, g_bank, late_bank, _, _ = banks(gf)
                for part, t, g in schedule_of("scalar", ga, gf):
                    if part == ("V" if gf else "VS"):
                        act.wait_ge(v_proj, g.tiles(t))
                        if not gf and t:
                            act.wait_ge(state_ps, g.states(t))
                        act.activation(v[:, :, 0:HD], v_bank.rearrange("p (h e) -> p h e", h=HEADS),
                                       ACT.Copy).then_inc(v_sb, 1)
                    elif part == "X1T":
                        act.wait_ge(x1T_ps, g.tiles(t))
                        src = late_bank[:, 0:D].rearrange("p (k n) -> p k n", k=KC)
                        act.activation(x1T[:, :, :], src, ACT.Copy).then_inc(x1T_sb, 1)
                        if t == 0 and positive(g.before(2).experts(NE - 1)):
                            act.wait_ge(h3_ps, g.before(2).experts(NE - 1))
                        act.activation(x1_h[:, g.p, :, t * P:(t + 1) * P], src, ACT.Copy).then_inc(x1T_high, 1)
                    elif part == ("G" if gf else "GS"):
                        act.wait_ge(g_proj, g.tiles(t))
                        if positive(g.tiles(t - 1)):
                            act.wait_ge(gated_sb, g.tiles(t - 1, HG))
                        act.activation(gate[:, :], g_bank, ACT.Silu).then_inc(gate_sb, 1)
                    elif part == "LOGITS" and t == TPG - 1:
                        act.wait_ge(offset_sb, g.groups())
                        act.activation(share[:, :, :], offset[:, :, :], ACT.Tanh).then_inc(share_sb, 1)
                    elif part == "QKT":
                        act.wait_ge(qkT_ps, g.tiles(t))
                        if positive(g.tiles(t - 1)):
                            act.wait_ge(out_ps, g.tiles(t - 1))
                        act.activation(qkT[:, :, :], A[:, 2, :].rearrange("p (k n) -> p k n", k=4),
                                       ACT.Copy).then_inc(qkT_sb, 1)
                        if gf:
                            next_x(g, t)
                    elif part == "XS":
                        split_x(g, t)
                    elif part == "OUT":
                        act.wait_ge(out_ps, g.tiles(t))
                        if positive(g.tiles(t - 1)):
                            act.wait_ge(meansq_sb, g.tiles(t - 1))
                        act.activation(squares[:, :, :].rearrange("p (m r) e -> p m (r e)", m=HG), A[:, 2:4, 0:OW],
                                       ACT.Square, scale=float(HD) ** -0.5).then_inc(sq_sb, 1)
                    elif part == "WEIGHT":
                        weight(t)
                    elif part == "YT":
                        act.wait_ge(yT_ps, g.tiles(t))
                        act.activation(yT_h[:, :, :], late_bank.rearrange("p (k n) -> p k n", k=VC),
                                       ACT.Copy).then_inc(yT_high, 1)
                    elif part == "H1":
                        act.wait_ge(h1_ps, g.experts(t))
                        if positive(g.experts(t - 1)):
                            act.wait_ge(hid_sb, g.experts(t - 1))
                        act.activation(act1[:, :], F[:, 0, :], ACT.Silu).then_inc(act1_sb, 1)
                    elif part == "H3":
                        act.wait_ge(hid_sb, g.experts(t))
                        if positive(g.down(t - 2)):
                            act.wait_ge(ffn_ps, g.down(t - 2))
                        act.activation(hid_h[:, t % 2, :], hid[:, t % 2, :], ACT.Copy).then_inc(hid_high, 1)

            whole_run(act, group)

        @block.gpsimd
        def _(pool):
            def split_x(g, t):
                pool.wait_ge(x_high, g.tiles(t))
                if positive(g.tiles(t - 2)):
                    pool.wait_ge(g_proj, g.tiles(t - 2))
                pool.tensor_tensor(x_l[:, t % 2, :, :], xraw[:, g.p, :, t * P:(t + 1) * P],
                                   x_h[:, t % 2, :, :].bitcast(f32), ALU.subtract).then_inc(x_low, 1)

            def next_x(g, t):
                if t < TPG - 1:
                    split_x(g, t + 1)
                else:
                    split_x(Group(g.b, g.at + 1), 0)

            def group(ga, gf):
                for part, t, g in schedule_of("gpsimd", ga, gf):
                    c = TPG * g.p + t
                    if part == "XS":
                        split_x(g, t)
                    if part == "QK":
                        pool.wait_ge(qk_scaled, g.tiles(t))
                        if positive(g.tiles(t - 1)):
                            pool.wait_ge(qk_rot, g.tiles(t - 1))
                        src = qk_s[:, :].rearrange("p (h k) -> p h k", k=KD)
                        dst = qk_w[:, :].rearrange("p (h k) -> p h k", k=KD)
                        half = KD // 2
                        for lo, hi in ((0, half), (half, KD)):
                            s = sin[:, c:c + 1, lo:hi].to_broadcast([P, 2 * HEADS, half])
                            pool.tensor_tensor(dst[:, :, lo:hi], src[:, :, half - lo:KD - lo], s,
                                               ALU.mult).then_inc(qk_sin, 1)
                    elif part == "QKT":
                        next_x(g, t)
                    elif part == "OUT":
                        pool.wait_ge(meansq_sb, g.tiles(t))
                        if positive(g.tiles(t - 1)):
                            pool.wait_ge(y_sb, g.tiles(t - 1))
                        pool.tensor_tensor(rms[:, :], meansq[:, :], minus_half[:, :], ALU.pow).then_inc(rms_sb, 1)
                    elif part == "WO":
                        pool.wait_ge(var_sb, g.tiles(t))
                        if positive(g.tiles(t - 1)):
                            pool.wait_ge(x1_sb, g.tiles(t - 1))
                        pool.tensor_tensor(rstd[:, :], var_eps[:, :], minus_half[:, 0:1], ALU.pow).then_inc(rstd_sb, 1)
                    elif part == "H3":
                        pool.wait_ge(hid_high, g.experts(t))
                        if positive(g.down(t - 2)):
                            pool.wait_ge(ffn_ps, g.down(t - 2))
                        pool.tensor_tensor(hid_l[:, t % 2, :], hid[:, t % 2, :], hid_h[:, t % 2, :].bitcast(f32),
                                           ALU.subtract).then_inc(hid_low, 1)
                    elif part == "W" and t == NE - 1:
                        pool.wait_ge(var2_sb, g.groups())
                        pool.tensor_tensor(rstd2[:, :], var_eps2[:, :], minus_half[:, 0:TPG], ALU.pow)\
                            .then_inc(rstd2_sb, 1)

            pool.memset(minus_half[:, :], -0.5).then_inc(ready0, 1)
            pool.memset(v[:, :, HD:HE], 1.0).then_inc(ready0, 1)
            pool.memset(logits[:, :, EXPERTS:], PAD).then_inc(ready0, 1)
            pool.memset(top2[:, :, 2:8], PAD).then_inc(ready0, 1)
            pool.wait_ge(ready0, 4)
            whole_run(pool, group)

        @block.vector
        def _(dve):
            def weight(n):
                _, width, high, low = parts[n]
                dve.wait_ge(w_high, n + 1)
                dve.tensor_tensor(low, stage[n % len(stage)][:, 0:width], high.bitcast(f32), ALU.subtract).then_inc(w_low, 1)

            def group(ga, gf):
                qk_bank, _, _, late_bank, wo_bank, logits_bank = banks(gf)
                for part, t, g in schedule_of("vector", ga, gf):
                    c = TPG * g.p + t
                    if part == "QK":
                        dve.wait_ge(qk_proj, g.tiles(t))
                        if g.first() and t == 0:
                            dve.wait_ge(s_cst, 16)
                        if positive(g.tiles(t - 1)):
                            dve.wait_ge(qk_sin, g.tiles(t - 1, 2))
                        heads = lambda a: a.rearrange("p (h k) -> p h k", k=KD)
                        dve.tensor_tensor(heads(qk_s[:, :]), heads(qk_bank),
                                          gamma.unsqueeze(2).to_broadcast([P, 2 * HEADS, KD]),
                                          ALU.mult).then_inc(qk_scaled, 1)
                        dve.wait_ge(qk_scaled, g.tiles(t))
                        dve.tensor_tensor(heads(qk_c[:, :]), heads(qk_s[:, :]),
                                          cos[:, c:c + 1, :].to_broadcast([P, 2 * HEADS, KD]),
                                          ALU.mult).then_inc(qk_cos, 1)
                    elif part == "ROT":
                        dve.wait_ge(qk_cos, g.tiles(t))
                        dve.wait_ge(qk_sin, g.tiles(t, 2))
                        dve.tensor_tensor(qk[:, t % 2, :], qk_c[:, :], qk_w[:, :], ALU.add).then_inc(qk_rot, 1)
                    elif part == "X1T":
                        dve.wait_ge(x1T_high, g.tiles(t))
                        cut = slice(t * P, (t + 1) * P)
                        dve.tensor_tensor(x1_l[:, g.p, :, cut], late_bank[:, 0:D].rearrange("p (k n) -> p k n", k=KC),
                                          x1_h[:, g.p, :, cut].bitcast(f32), ALU.subtract).then_inc(x1T_low, 1)
                    elif part == "LOGITS":
                        dve.wait_ge(logits_ps, g.tiles(t))
                        if g.first() and t == 0:
                            dve.wait_ge(s_router, 32)
                        dve.tensor_tensor(logits[:, t, 0:EXPERTS], logits_bank, br[:, :],
                                          ALU.add).then_inc(logits_sb, 1)
                        if t == TPG - 1:
                            route(g)
                    elif part == "SCORES":
                        dve.wait_ge(scores_ps, g.tiles(t))
                        for m in (1, 0):
                            dve.tensor_tensor(
                                scores[:, 2 * m:2 * m + 2, :, :].rearrange("p b m n -> p (b m) n"),
                                A[:, 2 * m:2 * m + 2, 0:2 * P].rearrange("p b (m n) -> p b m n", m=2),
                                causal.unsqueeze(1).to_broadcast([P, 4, P]), ALU.mult).then_inc(scores_sb, 1)
                    elif part == "OUT":
                        retention_out(g, t, c)
                    elif part == "WEIGHT":
                        weight(t)
                    elif part == "NORM":
                        retention_norm(g, t)
                    elif part == "YT":
                        dve.wait_ge(yT_high, g.tiles(t))
                        dve.tensor_tensor(yT_l[:, :, :], late_bank.rearrange("p (k n) -> p k n", k=VC),
                                          yT_h[:, :, :].bitcast(f32), ALU.subtract).then_inc(yT_low, 1)
                    elif part == "WO":
                        layer_norm(g, t, wo_bank)
                    elif part == "X1":
                        layer_norm_apply(g, t)
                    elif part == "H3":
                        dve.wait_ge(act1_sb, g.experts(t))
                        dve.wait_ge(h3_ps, g.experts(t))
                        if positive(g.experts(max(t - 2, -1))):
                            dve.wait_ge(hid_low, g.experts(max(t - 2, -1)))
                        dve.tensor_tensor(hid[:, t % 2, :], F[:, 1, :], act1[:, :], ALU.mult).then_inc(hid_sb, 1)
                    elif part in ("SUM1", "SUM2"):
                        add_expert(g, t, 0 if part == "SUM1" else 1)
                        if (part, t) == ("SUM2", NE - 1):
                            moments_out(g)
                    elif part == "RESULT":
                        layer_norm_out(g)

            def hold():
                dve.sem_inc(held, 1)

            def retention_out(g, t, c):
                four = lambda a: a.rearrange("p (r e) -> p r e", e=HE)
                if c < CHUNKS - 1:
                    dve.wait_ge(state_ps, g.states(c + 1))
                    if positive(g.states(c, HG)):
                        dve.wait_ge(state_sb, g.states(c, HG))
                    dve.tensor_tensor(state_new[:, :, :], A[:, 0:2, 0:OW], block_decay, ALU.mult)\
                        .then_inc(state_upd, 1)
                dve.wait_ge(sq_sb, g.tiles(t))
                dve.tensor_reduce(sumsq[:, :], squares[:, :, 0:HD], AX.X, ALU.add).then_inc(norm_step, 1)
                dve.tensor_tensor(denom[:, :], squares[:, :, HD], rowsum[:, c, :], ALU.max).then_inc(norm_step, 1)
                dve.wait_ge(norm_step, g.tiles(t, 2))
                dve.scalar_tensor_tensor(meansq[:, :], denom[:, :], HD * EPS, sumsq[:, :], ALU.mult,
                                         ALU.add).then_inc(meansq_sb, 1)
                dve.wait_ge(gate_sb, g.tiles(t))
                for m in range(HG):
                    dve.tensor_tensor(gated[:, m * 4 * HD:(m + 1) * 4 * HD].rearrange("p (r e) -> p r e", e=HD),
                                      four(A[:, 2 + m, 0:OW])[:, :, 0:HD],
                                      gate[:, m * 4 * HD:(m + 1) * 4 * HD].rearrange("p (r e) -> p r e", e=HD),
                                      ALU.mult).then_inc(gated_sb, 1)
                if c < CHUNKS - 1:
                    dve.wait_ge(state_upd, g.states(c + 1))
                    if c == 0:
                        dve.tensor_copy(state[:, :, :], state_new[:, :, :]).then_inc(state_sb, HG)
                    else:
                        for m in range(HG):
                            dve.scalar_tensor_tensor(state[:, m, :], state[:, m, :], gamma_chunk[:, m:m + 1],
                                                     state_new[:, m, :], ALU.mult, ALU.add).then_inc(state_sb, 1)

            def retention_norm(g, t):
                dve.wait_ge(rms_sb, g.tiles(t))
                dve.wait_ge(gated_sb, g.tiles(t, HG))
                dve.tensor_tensor(y[:, :].rearrange("p (h e) -> p h e", e=HD),
                                  gated[:, :].rearrange("p (h e) -> p h e", e=HD),
                                  rms[:, :].unsqueeze(2).to_broadcast([P, HEADS, HD]), ALU.mult).then_inc(y_sb, 1)

            def layer_norm(g, t, wo_bank):
                dve.wait_ge(wo_ps, g.tiles(t))
                if t == 0:
                    dve.wait_ge(s_x[g.p], g.rows(16))
                dve.tensor_tensor(res[:, :], wo_bank, xres[:, g.p, t, :], ALU.add).then_inc(ln_step, 1)
                dve.wait_ge(ln_step, g.tiles(t, 3) - 2)
                dve.bn_stats(stats[:, :], res[:, :]).then_inc(ln_step, 1)
                dve.wait_ge(ln_step, g.tiles(t, 3) - 1)
                hold()
                dve.bn_aggr(moments[:, :], stats[:, :]).then_inc(ln_step, 1)
                dve.wait_ge(ln_step, g.tiles(t, 3))
                dve.tensor_scalar(var_eps[:, :], moments[:, 1:2], EPS, None, ALU.add).then_inc(var_sb, 1)

            def layer_norm_apply(g, t):
                dve.wait_ge(rstd_sb, g.tiles(t))
                if t == 0 and positive(g.groups(16, -1)):
                    dve.wait_ge(s_out, g.groups(16, -1))
                dve.tensor_scalar(x1[:, g.p, t, :], res[:, :], moments[:, 0:1], rstd[:, :], ALU.subtract,
                                  ALU.mult).then_inc(x1_sb, 1)

            def route(g):
                n = lambda k: g.groups(2 * TPG + 6, 0) + k
                dve.wait_ge(logits_sb, g.tiles(TPG - 1))
                hold()
                for s in range(TPG):
                    dve.max(top8[:, s, :], logits[:, s, 0:EXPERTS]).then_inc(route_step, 1)
                dve.wait_ge(route_step, n(TPG))
                dve.tensor_copy(top2[:, :, 0:2], top8[:, :, 0:2]).then_inc(route_step, 1)
                dve.tensor_tensor(middle[:, :], top8[:, :, 0], top8[:, :, 1], ALU.add).then_inc(route_step, 1)
                dve.wait_ge(route_step, n(TPG + 2))
                dve.scalar_tensor_tensor(offset[:, :, :], middle[:, :].unsqueeze(2).to_broadcast([P, TPG, EXPERTS]),
                                         -0.5, logits[:, :, 0:EXPERTS], ALU.mult, ALU.add).then_inc(offset_sb, 1)
                for s in range(TPG):
                    dve.match_replace(without[:, s, :], top2[:, s, :], logits[:, s, :], -PAD).then_inc(route_step, 1)
                dve.wait_ge(route_step, n(2 * TPG + 2))
                dve.tensor_tensor(chosen[:, :, :], logits[:, :, 0:EXPERTS], without[:, :, 0:EXPERTS],
                                  ALU.not_equal).then_inc(route_step, 1)
                dve.wait_ge(share_sb, g.groups())
                dve.tensor_scalar(half_share[:, :, :], share[:, :, :], 0.5, 0.5, ALU.mult, ALU.add)\
                    .then_inc(route_step, 1)
                dve.wait_ge(route_step, n(2 * TPG + 4))
                dve.tensor_tensor(gates[:, g.p, :, :], half_share[:, :, :], chosen[:, :, :], ALU.mult)\
                    .then_inc(route_step, 2)

            def add_expert(g, i, half):
                dve.wait_ge(ffn_ps, g.down(i) - 1 + half if i > 1 else g.down(i) - 2 + 2 * half)
                if i == 1:
                    acc = x1[:, g.p, 2 * half:2 * half + 2, :].rearrange("p t d -> p (t d)")
                    dve.tensor_tensor(acc, F[:, 2 + half, :], acc, ALU.add).then_inc(sum_sb, 4)
                    return
                if i == 2 and not half:
                    dve.wait_ge(route_step, g.groups(2 * TPG + 6))
                for s in (2 * half, 2 * half + 1):
                    dve.wait_ge(sum_sb, g.experts(1, 4) - 4 + 4 * half if i == 2 else g.experts(i - 1, 4) + s + 1 - TPG)
                    dve.scalar_tensor_tensor(x1[:, g.p, s, :], F[:, 2 + half, (s % 2) * D:(s % 2 + 1) * D],
                                             gates[:, g.p, s, i - SHARED:i - SHARED + 1], x1[:, g.p, s, :],
                                             ALU.mult, ALU.add).then_inc(sum_sb, 1)

            def moments_out(g):
                for s in range(TPG):
                    dve.wait_ge(sum_sb, g.experts(NE - 1, 4) + s + 1 - TPG)
                    dve.bn_stats(stats2[:, s, :], x1[:, g.p, s, :]).then_inc(ln2_step, 1)
                for s in range(TPG):
                    dve.wait_ge(ln2_step, g.groups(2 * TPG, 0) + s + 1)
                    hold()
                    dve.bn_aggr(moments2[:, s, :], stats2[:, s, :]).then_inc(ln2_step, 1)
                dve.wait_ge(ln2_step, g.groups(2 * TPG))
                dve.tensor_scalar(var_eps2[:, :], moments2[:, :, 1], EPS, None, ALU.add).then_inc(var2_sb, 1)

            def layer_norm_out(g):
                dve.wait_ge(rstd2_sb, g.groups())
                for s in range(TPG):
                    dve.tensor_scalar(x1[:, g.p, s, :], x1[:, g.p, s, :], moments2[:, s, 0:1], rstd2[:, s:s + 1],
                                      ALU.subtract, ALU.mult).then_inc(result_sb, 1)

            dve.wait_ge(ready0, 4)
            whole_run(dve, group)


def shape_constants():
    f = np.float32
    lin = np.linspace(0.0, 1.0, KD // 2).astype(f)
    angle = (f(1.0) / np.power(f(10000.0), lin)).astype(f)
    pos = np.arange(SEQ, dtype=f)
    arg = (pos[:, None] * angle[None, :]).astype(f).astype(np.float64)
    s, c = np.sin(arg), np.cos(arg)
    decay = np.log1p(-2.0 ** (-5.0 - np.arange(HEADS, dtype=np.float64)))
    i = np.arange(P, dtype=np.float64)
    t = {}
    grow = np.exp(i[:, None] * decay[None, :])
    t["gamma"] = np.concatenate([grow, float(KD) ** -0.5 / grow], 1)
    by_chunk = lambda a: a.reshape(CHUNKS, P, -1).transpose(1, 0, 2).reshape(P, -1)
    t["cos"] = by_chunk(np.concatenate([c, c], 1))
    t["sin"] = by_chunk(np.concatenate([-s, s], 1))
    t["causal"] = (i[:, None] <= i[None, :]).astype(np.float64)
    block = np.zeros((P, HG, OW))
    per_chunk = np.exp(P * decay)
    for h in range(HEADS):
        m, r = h // 4, h % 4
        block[r * KD:(r + 1) * KD, m, r * HE:(r + 1) * HE] = per_chunk[h]
    t["block"] = block.reshape(P, -1)
    t["gamma_chunk"] = np.repeat(per_chunk.reshape(HG, 4).T, KD, axis=0)
    rows = np.cumsum(np.exp(np.arange(SEQ)[:, None] * decay[None, :]), 0)
    t["rowsum"] = by_chunk(rows / HD)
    t["ident"] = np.eye(P)
    return np.concatenate([t[name].reshape(P, width) for name, width in CONST_WIDTHS], 1).astype(f)


def kernel(**inputs):
    import numpy as _np
    import concourse.bacc as _bacc
    from concourse import mybir as _mybir
    from concourse.bass_utils import run_bass_kernel_spmd as _run

    a = {k.removeprefix("L0_"): _np.asarray(v) for k, v in inputs.items()}
    x = a["attn_x"].reshape(BATCH * SEQ, D)
    even_odd = _np.arange(D).reshape(HEADS, KD // 2, 2).transpose(0, 2, 1).reshape(-1)
    rows = lambda w: w.reshape(-1, P, w.shape[-1]).transpose(1, 0, 2)
    flat = lambda w: rows(w).reshape(P, -1)
    qk = _np.concatenate([a["attn_wq"][:, even_odd], a["attn_wk"][:, even_odd]], 1)
    experts = [(a["ffn_shared_w1"][e], a["ffn_shared_w3"][e], a["ffn_shared_w2"][e]) for e in range(SHARED)]
    experts += [(a["ffn_routed_w1"][e], a["ffn_routed_w3"][e], a["ffn_routed_w2"][e]) for e in range(EXPERTS)]
    arrays = {
        "x": x,
        "xT": _np.concatenate([x, x[:GT]]).reshape(NG + 1, GT, KC, P).transpose(0, 3, 2, 1),
        "w_att": _np.stack([flat(w) for w in (qk, a["attn_wv"], a["attn_wg"])]),
        "w_wo": flat(a["attn_wo"]),
        "w_ffn": _np.stack([_np.concatenate([flat(m) for m in e], 1) for e in experts]),
        "w_router": rows(a["ffn_router_w"]),
        "b_router": _np.repeat(a["ffn_router_b"][None, :], P, 0),
        "consts": shape_constants(),
    }
    arrays = {k: _np.ascontiguousarray(v) for k, v in arrays.items()}

    nc = _bacc.Bacc("TRN2", target_bir_lowering=False, num_devices=1)
    args = [nc.dram_tensor(k, v.shape, _mybir.dt.from_np(v.dtype), kind="ExternalInput").ap()
            for k, v in arrays.items()]
    out = nc.dram_tensor("out", (BATCH * SEQ, D), _mybir.dt.float32, kind="ExternalOutput").ap()
    retention_moe_kernel(nc, *args, out)
    r = _run(nc, [arrays], core_ids=[0])
    return r.results[0]["out"].reshape(BATCH, SEQ, D)
```
